# Optimizing a Trainium2 kernel written in Bass

```python
import numpy as np
import jax
import jax.numpy as jnp

def _softmax(x, axis=-1):
    return jax.nn.softmax(x, axis=axis)

def _gelu(x):
    return jax.nn.gelu(x, approximate=True)

def _silu(x):
    return jax.nn.silu(x)

def _sigmoid(x):
    return jax.nn.sigmoid(x)

def _layernorm(x, axis=-1, eps=1e-05):
    m = jnp.mean(x, axis=axis, keepdims=True)
    v = jnp.var(x, axis=axis, keepdims=True)
    return (x - m) / jnp.sqrt(v + eps)

def _scatter_add(tgt, idx, src, axis=0):
    return tgt.at[idx].add(src)

def _segment_sum(src, seg, n):
    return jax.ops.segment_sum(src, seg, n)
kernel_name = 'mk_macaron_d1_jaxref_r8_652b7c'

def setup_inputs(seed: int=0):
    np.random.seed(seed)
    _w = jnp.asarray

    def _L0_attn_setup():
        import jax, jax.numpy as jnp
        import numpy as np
        import math
        B, S, DM = (1, 256, 512)
        H, HKV, HD = (32, 8, 128)
        EPS = 1e-06
        NEG_INF = -1e+30

        def _alibi_slopes(n_heads: int) -> np.ndarray:
            start = 2 ** (-2 ** (-(math.log2(n_heads) - 3)))
            return np.array([start * start ** i for i in range(n_heads)], dtype=np.float32)

        def _rmsnorm(t, w):
            tf = t.astype(jnp.float32)
            inv = jax.lax.rsqrt(jnp.mean(tf * tf, axis=-1, keepdims=True) + EPS)
            return (tf * inv * w).astype(t.dtype)
        key = jax.random.key(seed)
        ks = jax.random.split(key, 5)
        std = 0.02
        return {'x': jax.random.normal(ks[0], (B, S, DM), dtype=jnp.float32), 'Wq': jax.random.normal(ks[1], (H * HD, DM), dtype=jnp.float32) * std, 'Wk': jax.random.normal(ks[2], (HKV * HD, DM), dtype=jnp.float32) * std, 'Wv': jax.random.normal(ks[3], (HKV * HD, DM), dtype=jnp.float32) * std, 'Wo': jax.random.normal(ks[4], (H * HD, DM), dtype=jnp.float32).T * (std / math.sqrt(2 * 32)), 'q_norm_w': jnp.ones((HD,), dtype=jnp.float32), 'k_norm_w': jnp.ones((HD,), dtype=jnp.float32)}
    _L0_attn_in = _L0_attn_setup()

    def _L0_ffn_setup():
        import jax, jax.numpy as jnp
        import numpy as np
        B, S, H, I, R = (4, 32, 512, 1792, 4)

        def _anemll_linear(x, w, su, sv):
            w_eff = w * (su @ sv)
            return jnp.einsum('bsh,oh->bso', x, w_eff)
        key = jax.random.key(seed)
        ks = jax.random.split(key, 10)
        sd = 0.02
        return {'x': jax.random.normal(ks[0], (B, S, H), dtype=jnp.float32), 'gate_w': jax.random.normal(ks[1], (I, H), dtype=jnp.float32) * sd, 'gate_su': jax.random.normal(ks[2], (I, R), dtype=jnp.float32) * 0.5, 'gate_sv': jax.random.normal(ks[3], (R, H), dtype=jnp.float32) * 0.5, 'up_w': jax.random.normal(ks[4], (I, H), dtype=jnp.float32) * sd, 'up_su': jax.random.normal(ks[5], (I, R), dtype=jnp.float32) * 0.5, 'up_sv': jax.random.normal(ks[6], (R, H), dtype=jnp.float32) * 0.5, 'down_w': jax.random.normal(ks[7], (H, I), dtype=jnp.float32) * sd, 'down_su': jax.random.normal(ks[8], (H, R), dtype=jnp.float32) * 0.5, 'down_sv': jax.random.normal(ks[9], (R, I), dtype=jnp.float32) * 0.5}
    _L0_ffn_in = _L0_ffn_setup()
    _d = {'L0_attn_x': _L0_attn_in['x'], 'L0_attn_Wq': _L0_attn_in['Wq'], 'L0_attn_Wk': _L0_attn_in['Wk'], 'L0_attn_Wv': _L0_attn_in['Wv'], 'L0_attn_Wo': _L0_attn_in['Wo'], 'L0_attn_q_norm_w': _L0_attn_in['q_norm_w'], 'L0_attn_k_norm_w': _L0_attn_in['k_norm_w'], 'L0_ffn_gate_w': _L0_ffn_in['gate_w'], 'L0_ffn_gate_su': _L0_ffn_in['gate_su'], 'L0_ffn_gate_sv': _L0_ffn_in['gate_sv'], 'L0_ffn_up_w': _L0_ffn_in['up_w'], 'L0_ffn_up_su': _L0_ffn_in['up_su'], 'L0_ffn_up_sv': _L0_ffn_in['up_sv'], 'L0_ffn_down_w': _L0_ffn_in['down_w'], 'L0_ffn_down_su': _L0_ffn_in['down_su'], 'L0_ffn_down_sv': _L0_ffn_in['down_sv']}
    _x0 = _d['L0_attn_x']
    _d['L0_attn_x'] = jax.random.normal(jax.random.fold_in(jax.random.key(seed), 1), (2, 512, 512), dtype=_x0.dtype)
    del _x0
    return _d

def reference(L0_attn_x, L0_attn_Wq, L0_attn_Wk, L0_attn_Wv, L0_attn_Wo, L0_attn_q_norm_w, L0_attn_k_norm_w, L0_ffn_gate_w, L0_ffn_gate_su, L0_ffn_gate_sv, L0_ffn_up_w, L0_ffn_up_su, L0_ffn_up_sv, L0_ffn_down_w, L0_ffn_down_su, L0_ffn_down_sv):

    def _L0_attn_ref(x, Wq, Wk, Wv, Wo, q_norm_w, k_norm_w):
        import jax, jax.numpy as jnp
        import numpy as np
        import math
        B, S, DM = (1, 256, 512)
        H, HKV, HD = (32, 8, 128)
        EPS = 1e-06
        NEG_INF = -1e+30

        def _alibi_slopes(n_heads: int) -> np.ndarray:
            start = 2 ** (-2 ** (-(math.log2(n_heads) - 3)))
            return np.array([start * start ** i for i in range(n_heads)], dtype=np.float32)

        def _rmsnorm(t, w):
            tf = t.astype(jnp.float32)
            inv = jax.lax.rsqrt(jnp.mean(tf * tf, axis=-1, keepdims=True) + EPS)
            return (tf * inv * w).astype(t.dtype)
        b, s, _ = x.shape
        G = H // HKV
        q = (x @ Wq.T).reshape(b, s, H, HD).transpose(0, 2, 1, 3)
        k = (x @ Wk.T).reshape(b, s, HKV, HD).transpose(0, 2, 1, 3)
        v = (x @ Wv.T).reshape(b, s, HKV, HD).transpose(0, 2, 1, 3)
        q = _rmsnorm(q, q_norm_w)
        k = _rmsnorm(k, k_norm_w)
        qg = q.reshape(b, HKV, G, s, HD)
        scores = jnp.einsum('bkgqd,bksd->bkgqs', qg, k) / math.sqrt(HD)
        slopes = jnp.asarray(_alibi_slopes(H)).reshape(HKV, G)
        pos = jnp.arange(s, dtype=jnp.float32)
        rel = pos[None, :] - pos[:, None]
        bias = jnp.where(rel > 0, NEG_INF, slopes[:, :, None, None] * rel)
        attn = jax.nn.softmax(scores + bias[None], axis=-1)
        out = jnp.einsum('bkgqs,bksd->bkgqd', attn, v)
        out = out.reshape(b, H, s, HD).transpose(0, 2, 1, 3).reshape(b, s, H * HD)
        return out @ Wo.T

    def _L0_ffn_ref(x, gate_w, gate_su, gate_sv, up_w, up_su, up_sv, down_w, down_su, down_sv):
        import jax, jax.numpy as jnp
        import numpy as np
        B, S, H, I, R = (4, 32, 512, 1792, 4)

        def _anemll_linear(x, w, su, sv):
            w_eff = w * (su @ sv)
            return jnp.einsum('bsh,oh->bso', x, w_eff)
        a = _anemll_linear(x, gate_w, gate_su, gate_sv)
        b = _anemll_linear(x, up_w, up_su, up_sv)
        d = jax.nn.silu(a) * b
        return _anemll_linear(d, down_w, down_su, down_sv)
    x = L0_attn_x
    x = x + 0.5 * _L0_ffn_ref(_layernorm(x, axis=-1), L0_ffn_gate_w, L0_ffn_gate_su, L0_ffn_gate_sv, L0_ffn_up_w, L0_ffn_up_su, L0_ffn_up_sv, L0_ffn_down_w, L0_ffn_down_su, L0_ffn_down_sv)
    x = x + _L0_attn_ref(_layernorm(x, axis=-1), L0_attn_Wq, L0_attn_Wk, L0_attn_Wv, L0_attn_Wo, L0_attn_q_norm_w, L0_attn_k_norm_w)
    x = x + 0.5 * _L0_ffn_ref(_layernorm(x, axis=-1), L0_ffn_gate_w, L0_ffn_gate_su, L0_ffn_gate_sv, L0_ffn_up_w, L0_ffn_up_su, L0_ffn_up_sv, L0_ffn_down_w, L0_ffn_down_su, L0_ffn_down_sv)
    return x

_drawn_inputs = setup_inputs


def setup_inputs(seed=0):
    import zlib

    import numpy as np

    out = dict(_drawn_inputs(seed))
    spreads = {'L0_attn_q_norm_w': (1.0, 0.2), 'L0_attn_k_norm_w': (1.0, 0.2)}
    factors = {}
    for name, (base, spread) in spreads.items():
        noise = np.random.default_rng([zlib.crc32(name.encode()), seed]).standard_normal(out[name].shape)
        drawn = base * np.exp(spread * noise) if base else spread * noise
        out[name] = jnp.asarray(drawn.astype(out[name].dtype))
    for name, factor in factors.items():
        out[name] = (out[name] * factor).astype(out[name].dtype)
    return out
```

```python
from contextlib import ExitStack, contextmanager

import numpy as np

import concourse.bass as bass
from concourse import mybir

F32, F32R, I32 = mybir.dt.float32, mybir.dt.float32r, mybir.dt.int32
ALU = mybir.AluOpType
ACT = mybir.ActivationFunctionType
AX = mybir.AxisListType

P = 128
BANKS = 8
B, S, DM = 2, 512, 512
KC = DM // P
TB = S // P
H, HKV, HD = 32, 8, 128
G = H // HKV
QW = G * HD
QKW = QW + HD
QKVW = QKW + HD
FI = 1792
R = 4
CH = 2
STEPS = FI // P // CH
LN_EPS, RMS_EPS = 1e-5, 1e-6
MASKED = -1e30
ROOT_MAGIC = 1597463007.0
SLOPE0 = 2 ** -(2 ** -(np.log2(H) - 3))
assert abs(SLOPE0 ** G - 0.5) < 1e-12


class Mark:

    def __init__(self, count):
        self.count = count


class Tally:

    def __init__(self, sem, per):
        self.sem, self.per = sem, per
        self.count, self.loop, self.made = 0, None, []

    def mark(self, instruction, by=1, spare=0):
        instruction.then_inc(self.sem, by + spare)
        m = Mark(self.count + by)
        self.count += by + spare
        if self.loop:
            self.made.append(m)
        return m

    def wait(self, engine, until=None):
        count = self.count if until is None else until.count if isinstance(until, Mark) else until
        if self.loop:
            name, i = self.loop
            if name in self.per:
                count = i * self.per[name] + count
        elif count <= 0:
            return
        engine.wait_ge(self.sem, count)


def build(nc, x, ffn_w, ffn_fac, ffn_fix, w_qkv, w_o, norm_w, out):
    with ExitStack() as ctx:
        def sb(name, shape, dt=F32, stack=ctx):
            return stack.enter_context(nc.sbuf_tensor(name, [P, *shape], dt))

        tallies = []

        def tally(name, **per):
            t = Tally(ctx.enter_context(nc.semaphore(name)), per)
            tallies.append(t)
            return t

        @contextmanager
        def loop(name, n):
            with nc.Fori(0, n) as i:
                starts = [t.count for t in tallies]
                for t in tallies:
                    t.loop, t.made = (name, i), []
                yield i
                for t, start in zip(tallies, starts):
                    per = t.count - start
                    assert per == t.per.get(name, 0), (name, t.sem.name, per)
                    t.count += (n - 1) * per
                    t.loop = None
                    for m in t.made:
                        m.count += (n - 1) * per

        pe, act, dve, pool, sp = nc.tensor, nc.scalar, nc.vector, nc.gpsimd, nc.sync
        banks = [ctx.enter_context(nc.psum_tensor(f"bank{i}", [P, 512], F32)) for i in range(BANKS)]

        PAIRS = B * G
        FFN_SPLITS = 2 * (2 * CH - CH + 1)
        FFN_RESULTS = 2 * CH * B + TB * B + FFN_SPLITS
        FFN_SPARE = -FFN_RESULTS % BANKS
        PROB_RESULTS = 3
        ATT_RESULTS = B * (2 * TB + 1) + PAIRS * (1 + TB + PROB_RESULTS + 1) + PAIRS // 2 * TB
        ATT_SPARE = -ATT_RESULTS % BANKS
        KINDS = ("gu0", "gu1", "down")

        full = tally("full", ffn=FFN_RESULTS + FFN_SPARE, att=ATT_RESULTS + ATT_SPARE)
        evac = tally("evac", ffn=FFN_RESULTS + FFN_SPARE, att=ATT_RESULTS + ATT_SPARE)
        hi_done = tally("hi_done", ffn=2 * CH * B, att=PAIRS * (PROB_RESULTS + 2) + B + B * TB * 3)
        gated = tally("gated", ffn=CH * B)
        exp_done = tally("exp_done", att=PAIRS)
        top_done = tally("top_done", att=PAIRS)
        prob_done = tally("prob_done", att=PAIRS)
        root_done = tally("root_done", att=B)
        rows_done = tally("rows_done", att=B * TB)
        bias_done = tally("bias_done", att=G)
        own = tally("own", att=PAIRS + B * (TB + 10))
        w_hi = tally("w_hi", ffn=FFN_SPLITS, att=KC + G)
        w_lo = tally("w_lo", ffn=FFN_SPLITS, att=KC + G)
        fac_hi = tally("fac_hi", ffn=2 + 2 + 1)
        fac_done = tally("fac_done", ffn=len(KINDS))
        w_in = {k: tally(f"w_in_{k}", ffn=16) for k in KINDS} | {k: tally(f"w_in_{k}", att=16) for k in ("qkv", "o")}
        fac_in = {k: tally(f"fac_in_{k}", ffn=16 * 4) for k in KINDS}
        x_in = [tally(f"x_in{t}") for t in range(B * TB)]
        norm_in = tally("norm_in")
        fix_in = tally("fix_in")
        ready = tally("ready")
        xn_done = tally("xn_done")
        x_out = tally("x_out")

        passed = ctx.enter_context(nc.semaphore("passed"))

        def settle(engine):
            engine.sem_inc(passed, 1)

        def next_bank(operand=Mark(0)):
            evac.wait(pe, max(full.count + 1, operand.count))
            return banks[full.count % BANKS]

        xr = sb("x_rows", [B * TB, DM])
        xnT_hi = sb("xnT_hi", [KC, B * S], F32R)
        xnT_lo = sb("xnT_lo", [KC, B * S], F32R)
        ident = sb("ident", [P])
        wcol = sb("wcol", [2])
        wkcol = sb("wkcol", [1])
        stats = sb("stats", [B * TB, 6])
        mv = sb("mv", [B * TB, 2])
        ROOTS = TB * (G + 1)
        root_m, root_y, root_a, root_b = (sb(f"root_{n}", [ROOTS]) for n in "myab")
        xn = sb("xn", [2, DM])

        def own_step(instruction):
            own.mark(instruction)
            own.wait(dve)

        def inverse_root(mean_square, eps, n, scale=1.0):
            m, y, a, b = (t[:, 0:n] for t in (root_m, root_y, root_a, root_b))
            own_step(dve.tensor_scalar(m, mean_square, scale, eps, ALU.mult, ALU.add))
            own_step(dve.tensor_scalar(y.bitcast(I32), m.bitcast(I32), -0.5, ROOT_MAGIC, ALU.mult, ALU.add))
            for newton in range(3):
                own_step(dve.scalar_tensor_tensor(a, y, -0.5, y, ALU.mult, ALU.mult))
                own_step(dve.tensor_tensor(b, a, m, ALU.mult))
                last = dve.scalar_tensor_tensor(y, b, 1.5, y, ALU.add, ALU.mult)
                if newton < 2:
                    own_step(last)
            return y, last

        def matmul3(bank, left, right, first, last):
            (lh, ll), (rh, rl) = left, right
            pe.matmul(bank, lh, rh, start=first, stop=False)
            pe.matmul(bank, lh, rl, start=False, stop=False)
            return pe.matmul(bank, ll, rh, start=False, stop=last)

        def split_result(n, src, hi, lo, scale=None, spare=0):
            full.wait(act, n)
            if scale is None:
                hi_done.mark(act.copy(hi, src))
            else:
                hi_done.mark(act.activation(hi, src, ACT.Copy, scale=scale))
            hi_done.wait(dve)
            if scale is None:
                last = dve.tensor_tensor(lo, src, hi.bitcast(F32), ALU.subtract)
            else:
                last = dve.scalar_tensor_tensor(lo, src, scale, hi.bitcast(F32), ALU.mult, ALU.subtract)
            return evac.mark(last, spare=spare)

        def fresh_memory(engine):
            for t in (full, evac, hi_done, gated, w_hi, w_lo, fac_done, prob_done, rows_done, bias_done):
                t.wait(engine)

        x_rows = x.rearrange("b (t p) c -> (b t) p c", p=P)
        for t in range(B * TB):
            x_in[t].mark(sp.dma_start(xr[:, t, :], x_rows[t]), 16)
        norm_in.mark(sp.dma_start(wcol[:, :], norm_w), 16)
        dve.sem_inc(evac.sem, BANKS)
        evac.count = BANKS
        ready.mark(pool.memset(ident[:, :], 0.0))
        ready.wait(pool)
        ready.mark(pool.affine_select(out=ident[:, :], in_=ident[:, :], compare_op=ALU.not_equal, fill=1.0,
                                      base=0, pattern=[[-1, P]], channel_multiplier=1))
        ready.wait(pe)
        norm_in.wait(dve)
        own_step(dve.tensor_scalar(wkcol[:, :], wcol[:, 1:2], float(HD) ** -0.5, None, ALU.mult))

        xn_ready = []

        def layer_norm():
            evac.wait(dve)
            for t in range(B * TB):
                x_in[t].wait(dve)
                last = dve.bn_stats(stats[:, t, :], xr[:, t, :])
            own_step(last)
            for t in range(B * TB):
                last = dve.bn_aggr(mv[:, t, :], stats[:, t, :])
            own_step(last)
            rows_done.wait(dve)
            rstd, last = inverse_root(mv[:, :, 1], LN_EPS, B * TB)
            own_step(last)
            turned = []

            def norm(t):
                if t >= 2:
                    full.wait(dve, turned[t - 2])
                xn_done.mark(dve.tensor_scalar(xn[:, t % 2, :], xr[:, t, :], mv[:, t, 0:1], rstd[:, t:t + 1],
                                               ALU.subtract, ALU.mult))

            norm(0)
            for t in range(B * TB):
                xn_done.wait(pe)
                bank = next_bank()
                for k in range(KC):
                    last = pe.transpose(bank[:, k * P:(k + 1) * P], xn[:, t % 2, k * P:(k + 1) * P], ident[:, :])
                turned.append(full.mark(last))
                if t + 1 < B * TB:
                    norm(t + 1)
                cols = slice(t * P, (t + 1) * P)
                split_result(turned[t], bank[:, :].rearrange("p (k c) -> p k c", k=KC), xnT_hi[:, :, cols], xnT_lo[:, :, cols])
            xn_ready.append(Mark(evac.count))

        LEFT, RIGHT = [slice(64, P)], [slice(32, 64), slice(96, P)]

        def split_factor(raw, stack, parts):
            settle(pool)
            fac_hi.mark(pool.tensor_copy(stack[:, :], raw[:, :]))
            fac_hi.wait(pool)
            lo_parts = [(rows, cols) for cols, lo_rows in parts for rows in lo_rows]
            for n, (rows, cols) in enumerate(lo_parts):
                last = pool.tensor_tensor(stack[rows, cols], raw[rows, cols], stack[rows, cols].bitcast(F32), ALU.subtract)
                if n < len(lo_parts) - 1:
                    fac_hi.mark(last)
                    fac_hi.wait(pool)
            done = fac_done.mark(last)
            fac_done.wait(pool)
            return done

        def ffn(tag):
            with ExitStack() as part_memory:
                def psb(name, shape, dt=F32):
                    return sb(name + tag, shape, dt, part_memory)

                COLS = dict(gu0=2 * DM, gu1=2 * DM, down=CH * DM)
                raw = {k: psb(f"raw_{k}", [n]) for k, n in COLS.items()}
                w_h = {k: psb(f"w_h_{k}", [n], F32R) for k, n in COLS.items()}
                w_l = {k: psb(f"w_l_{k}", [n], F32R) for k, n in COLS.items()}
                fac_raw = {k: psb(f"fac_raw_{k}", [2 * P]) for k in KINDS}
                fac = {k: psb(f"fac_{k}", [2 * P], F32R) for k in KINDS}
                fix_raw = psb("fix_raw", [3 * DM])
                fix = psb("fix", [3 * DM], F32R)
                silu = psb("silu", [CH, S])
                d = psb("d", [CH, S])
                d_hi = psb("d_hi", [CH, B, S], F32R)
                d_lo = psb("d_lo", [CH, B, S], F32R)
                fac_ready, w_ready, d_ready = {}, {}, {}

                def load(kind, step):
                    at = slice(step, step + 1) if isinstance(step, int) else bass.ds(step, 1)
                    w_lo.wait(sp)
                    settle(sp)
                    fac_done.wait(sp)
                    settle(sp)
                    k = KINDS.index(kind)
                    start = sum(COLS[name] for name in KINDS[:k])
                    for g in range(4):
                        fac_in[kind].mark(sp.dma_start(fac_raw[kind][32 * g:32 * g + R, :],
                                                       ffn_fac[at][:, k].rearrange("s r c -> r (s c)")), 16)
                    w_in[kind].mark(sp.dma_start(raw[kind][:, :],
                                                 ffn_w[at][:, :, start:start + COLS[kind]].rearrange("s p c -> p (s c)")), 16)

                def stack_factors(kind):
                    fac_in[kind].wait(pool)
                    full.wait(pool)
                    fac_ready[kind] = split_factor(fac_raw[kind], fac[kind], [(slice(0, 2 * P), LEFT if kind == "down" else RIGHT)])

                def scale_weights(kind, spare=0):
                    fac_done.wait(pe, fac_ready[kind])
                    for half in range(2):
                        bank = next_bank()
                        one = slice(half * P, (half + 1) * P)
                        if kind == "down":
                            last = pe.matmul(bank[:, :], fac[kind][:, one], fix[:, 2 * DM:3 * DM], start=True, stop=True)
                        else:
                            for k in range(KC):
                                rows = slice(half * DM + k * P, half * DM + (k + 1) * P)
                                last = pe.matmul(bank[:, k * P:(k + 1) * P], fix[:, rows], fac[kind][:, one],
                                                 start=True, stop=True, skip_group_check=True)
                        n = full.mark(last, spare=spare * half)
                        cols = slice(half * DM, (half + 1) * DM)
                        w_in[kind].wait(dve)
                        full.wait(dve, n)
                        evac.mark(dve.tensor_tensor(raw[kind][:, cols], bank[:, :], raw[kind][:, cols], ALU.mult), spare=spare * half)
                        evac.wait(act)
                        w_hi.mark(act.copy(w_h[kind][:, cols], raw[kind][:, cols]))
                        w_hi.wait(pool)
                        w_ready[kind] = w_lo.mark(pool.tensor_tensor(w_l[kind][:, cols], raw[kind][:, cols],
                                                                     w_h[kind][:, cols].bitcast(F32), ALU.subtract))

                def gate_up(c, b):
                    kind = f"gu{c}"
                    w_lo.wait(pe, w_ready[kind])
                    results = []
                    for half in range(2):
                        bank = next_bank(xn_ready[-1])
                        for k in range(KC):
                            w = slice(half * DM + k * P, half * DM + (k + 1) * P)
                            tokens = slice(b * S, (b + 1) * S)
                            last = matmul3(bank[:, :], (w_h[kind][:, w], w_l[kind][:, w]),
                                           (xnT_hi[:, k, tokens], xnT_lo[:, k, tokens]), k == 0, k == KC - 1)
                        results.append((full.mark(last), bank))
                    (n_a, bank_a), (n_b, bank_b) = results
                    full.wait(act, n_a)
                    hi_done.mark(act.activation(silu[:, c, :], bank_a[:, :], ACT.Silu))
                    hi_done.wait(dve)
                    full.wait(dve, n_b)
                    gated.mark(dve.tensor_tensor(d[:, c, :], bank_b[:, :], silu[:, c, :], ALU.mult))
                    gated.wait(act)
                    hi_done.mark(act.copy(d_hi[:, c, b, :], d[:, c, :]))
                    hi_done.wait(dve)
                    d_ready[b] = evac.mark(dve.tensor_tensor(d_lo[:, c, b, :], d[:, c, :], d_hi[:, c, b, :].bitcast(F32),
                                                             ALU.subtract), 2)

                def down(b):
                    w_lo.wait(pe, w_ready["down"])
                    for t in range(TB):
                        bank = next_bank(d_ready[b])
                        tokens = slice(t * P, (t + 1) * P)
                        for c in range(CH):
                            w = slice(c * DM, (c + 1) * DM)
                            last = matmul3(bank[:, :], (d_hi[:, c, b, tokens], d_lo[:, c, b, tokens]),
                                           (w_h["down"][:, w], w_l["down"][:, w]), c == 0, c == CH - 1)
                        full.wait(dve, full.mark(last))
                        row = xr[:, b * TB + t, :]
                        evac.mark(dve.scalar_tensor_tensor(row, bank[:, :], 0.5, row, ALU.mult, ALU.add))

                def step(i, more):
                    if more:
                        for kind in KINDS:
                            load(kind, i + 1)
                        for kind in KINDS:
                            stack_factors(kind)
                    gate_up(1, 0)
                    gate_up(0, 1)
                    if more:
                        scale_weights("gu0")
                    down(0)
                    gate_up(1, 1)
                    if more:
                        scale_weights("gu1")
                        gate_up(0, 0)
                    down(1)
                    if more:
                        scale_weights("down", FFN_SPARE)

                fresh_memory(pool)
                fresh_memory(act)
                fresh_memory(sp)
                for t in (*fac_raw.values(), fix_raw):
                    ready.mark(pool.memset(t[:, :], 0.0))
                ready.wait(sp)
                for g in range(4):
                    fix_in.mark(sp.dma_start(fix_raw[32 * g:32 * g + R, :], ffn_fix), 16)
                for kind in KINDS:
                    load(kind, 0)
                fix_in.wait(pool)
                fix_ready = split_factor(fix_raw, fix, [(slice(0, 2 * DM), LEFT), (slice(2 * DM, 3 * DM), RIGHT)])
                for kind in KINDS:
                    stack_factors(kind)
                layer_norm()
                for kind in KINDS:
                    scale_weights(kind)
                gate_up(0, 0)
                with loop("ffn", STEPS - 1) as i:
                    step(i, True)
                step(STEPS - 1, False)

        def attention():
            with ExitStack() as part_memory:
                def psb(name, shape, dt=F32):
                    return sb(name, shape, dt, part_memory)

                raw = {"qkv": psb("raw_qkv", [KC, QKVW]), "o": psb("raw_o", [G, DM])}
                w_h = {"qkv": psb("qkv_h", [KC, QKVW], F32R), "o": psb("o_h", [G, DM], F32R)}
                w_l = {"qkv": psb("qkv_l", [KC, QKVW], F32R), "o": psb("o_l", [G, DM], F32R)}
                rows = psb("rows", [B, TB, G + 1, HD])
                square = psb("square", [G + 1, HD])
                sums = psb("sums", [TB, G + 1])
                v_h, v_l = psb("v_h", [B, TB, HD], F32R), psb("v_l", [B, TB, HD], F32R)
                kT_h, kT_l = psb("kT_h", [B, S], F32R), psb("kT_l", [B, S], F32R)
                qT_h, qT_l = psb("qT_h", [2, S], F32R), psb("qT_l", [2, S], F32R)
                OFF = [P * i * (i + 1) // 2 for i in range(TB + 1)]
                prob = psb("prob", [2, OFF[TB]])
                probT_h, probT_l = psb("probT_h", [OFF[TB]], F32R), psb("probT_l", [OFF[TB]], F32R)
                oT_h, oT_l = psb("oT_h", [2, 2, S], F32R), psb("oT_l", [2, 2, S], F32R)
                bias = psb("bias", [G, S])
                distance = psb("distance", [S], I32)
                top, neg_top, total, inverse = (psb(n, [2, TB]) for n in ("top", "neg_top", "total", "inverse"))
                TURNS = [[(0, 0)], [(1, 0), (3, 3 * P)], [(2, 0)]]
                probT_at = {j: S * n + at for n, turn in enumerate(TURNS) for j, at in turn}
                assert len(TURNS) == PROB_RESULTS and TB == 4
                w_ready, bias_ready, oT_ready, q_ready, probT_ready = {}, {}, {}, [None], [None]

                def load(kind, step):
                    at = slice(step, step + 1) if isinstance(step, int) else bass.ds(step, 1)
                    w_lo.wait(sp)
                    settle(sp)
                    src = w_qkv if kind == "qkv" else w_o
                    w_in[kind].mark(sp.dma_start(raw[kind][:, :, :].rearrange("p k c -> p (k c)"),
                                                 src[at].rearrange("s p c -> p (s c)")), 16)

                def split_weights(kind):
                    w_in[kind].wait(act)
                    full.wait(act)
                    for k in range(KC if kind == "qkv" else G):
                        w_hi.mark(act.copy(w_h[kind][:, k, :], raw[kind][:, k, :]))
                        w_hi.wait(pool)
                        w_ready[kind] = w_lo.mark(pool.tensor_tensor(w_l[kind][:, k, :], raw[kind][:, k, :],
                                                                     w_h[kind][:, k, :].bitcast(F32), ALU.subtract))

                def project(b, t):
                    w_lo.wait(pe, w_ready["qkv"])
                    results = []
                    tokens = slice(b * S + t * P, b * S + (t + 1) * P)
                    for cols in (slice(0, QW), slice(QW, QKVW)):
                        bank = next_bank(xn_ready[-1])
                        for k in range(KC):
                            last = matmul3(bank[:, 0:cols.stop - cols.start], (xnT_hi[:, k, tokens], xnT_lo[:, k, tokens]),
                                           (w_h["qkv"][:, k, cols], w_l["qkv"][:, k, cols]), k == 0, k == KC - 1)
                        results.append((full.mark(last), bank))
                    (n_q, bank_q), (n_kv, bank_kv) = results
                    q, k = rows[:, b, t, 0:G, :], rows[:, b, t, G, :]
                    bank_q = bank_q[:, :].rearrange("p (h d) -> p h d", h=G)
                    full.wait(act, n_q)
                    q_copied = hi_done.mark(act.copy(q, bank_q))
                    full.wait(act, n_kv)
                    hi_done.mark(act.copy(k, bank_kv[:, 0:HD]))
                    hi_done.mark(act.copy(v_h[:, b, t, :], bank_kv[:, HD:2 * HD]))
                    hi_done.wait(dve, q_copied)
                    evac.mark(dve.tensor_tensor(square[:, 0:G, :], bank_q, q, ALU.mult))
                    hi_done.wait(dve)
                    dve.tensor_tensor(v_l[:, b, t, :], bank_kv[:, HD:2 * HD], v_h[:, b, t, :].bitcast(F32), ALU.subtract)
                    evac.mark(dve.tensor_tensor(square[:, G, :], bank_kv[:, 0:HD], k, ALU.mult))
                    evac.wait(dve)
                    own_step(dve.tensor_reduce(sums[:, t, :], square[:, :, :], AX.X, ALU.add))

                def norm_rows(b):
                    rows_done.wait(dve)
                    root, last = inverse_root(sums[:, :, :].rearrange("p t h -> p (t h)"), RMS_EPS, ROOTS, 1.0 / HD)
                    root_done.mark(last)
                    root_done.wait(pool)
                    for t in range(TB):
                        by = root[:, t * (G + 1):(t + 1) * (G + 1)].unsqueeze(2).to_broadcast([P, G + 1, HD])
                        rows_done.mark(pool.tensor_tensor(rows[:, b, t], rows[:, b, t], by, ALU.mult))

                def turn_rows(b, head, hi, lo, weight, spare=0):
                    rows_done.wait(pe)
                    bank = next_bank()
                    for t in range(TB):
                        last = pe.transpose(bank[:, t * P:(t + 1) * P], rows[:, b, t, head, :], ident[:, :])
                    return split_result(full.mark(last, spare=spare), bank[:, :], hi, lo, weight, spare)

                def turn_k(b):
                    turn_rows(b, G, kT_h[:, b, :], kT_l[:, b, :], wkcol[:, 0:1])

                def turn_q(b, h, spare=0):
                    q_ready[0] = turn_rows(b, h, qT_h[:, h % 2, :], qT_l[:, h % 2, :], wcol[:, 0:1], spare)

                def scores(b, h):
                    s = h % 2
                    for i in range(TB):
                        bank = next_bank(q_ready[0])
                        n_keys = (i + 1) * P
                        q = slice(i * P, (i + 1) * P)
                        last = matmul3(bank[:, 0:n_keys], (qT_h[:, s, q], qT_l[:, s, q]),
                                       (kT_h[:, b, 0:n_keys], kT_l[:, b, 0:n_keys]), True, True)
                        full.wait(dve, full.mark(last))
                        bias_done.wait(dve, bias_ready[h])
                        settle(dve)
                        evac.mark(dve.tensor_tensor_reduce(
                            prob[:, s, OFF[i]:OFF[i + 1]], bank[:, 0:n_keys], bias[:, h, S - n_keys:S], 1.0, MASKED,
                            ALU.add, ALU.max, top[:, s, i:i + 1]))
                    evac.wait(dve)
                    top_done.mark(dve.tensor_scalar(neg_top[:, s, :], top[:, s, :], -1.0, None, ALU.mult))

                def exponentials(h):
                    s = h % 2
                    top_done.wait(act)
                    for i in range(TB):
                        p = prob[:, s, OFF[i]:OFF[i + 1]]
                        last = act.activation(p, p, ACT.Exp, bias=neg_top[:, s, i:i + 1], accum_out=total[:, s, i:i + 1])
                    exp_done.mark(last)

                def probabilities(h):
                    s = h % 2
                    exp_done.wait(dve)
                    own_step(dve.reciprocal(inverse[:, s, :], total[:, s, :]))
                    for i in range(TB):
                        p = prob[:, s, OFF[i]:OFF[i + 1]]
                        last = dve.tensor_scalar(p, p, inverse[:, s, i:i + 1], None, ALU.mult)
                    prob_done.mark(last)

                def turn_probabilities(h):
                    s = h % 2
                    prob_done.wait(pe)
                    for n, turn in enumerate(TURNS):
                        bank = next_bank()
                        for j, at in turn:
                            for i in range(j, TB):
                                here = at + (i - j) * P
                                last = pe.transpose(bank[:, here:here + P], prob[:, s, OFF[i] + j * P:OFF[i] + (j + 1) * P], ident[:, :])
                        width = here + P
                        here = slice(n * S, n * S + width)
                        probT_ready[0] = split_result(full.mark(last), bank[:, 0:width], probT_h[:, here], probT_l[:, here])

                def weigh_values(b, h):
                    bank = next_bank(probT_ready[0])
                    for j in range(TB):
                        width = S - j * P
                        here = slice(probT_at[j], probT_at[j] + width)
                        last = matmul3(bank[:, j * P:S], (v_h[:, b, j, :], v_l[:, b, j, :]),
                                       (probT_h[:, here], probT_l[:, here]), j == 0, j == TB - 1)
                    half = h // 2
                    oT_ready[half] = split_result(full.mark(last), bank[:, :], oT_h[:, half, h % 2, :], oT_l[:, half, h % 2, :])

                def project_out(b, half, blocks, spare=0):
                    w_lo.wait(pe, w_ready["o"])
                    for t in blocks:
                        bank = next_bank(oT_ready[half])
                        tokens = slice(t * P, (t + 1) * P)
                        for n in range(2):
                            h = 2 * half + n
                            last = matmul3(bank[:, :], (oT_h[:, half, n, tokens], oT_l[:, half, n, tokens]),
                                           (w_h["o"][:, h, :], w_l["o"][:, h, :]), n == 0, n == 1)
                        spared = spare if t == blocks[-1] else 0
                        full.wait(dve, full.mark(last, spare=spared))
                        row = xr[:, b * TB + t, :]
                        evac.mark(dve.tensor_tensor(row, bank[:, :], row, ALU.add), spare=spared)

                PROJECT = [(0, 1), (2,), (3,), ()]
                OUT = {3: (0, 0, (0, 1)), 4: (0, 0, (2, 3)), 5: (0, 1, (0, 1)), 6: (0, 1, (2, 3)), 7: (1, 0, (0, 1))}

                def group(g, more):
                    if more:
                        load("qkv", g + 1)
                    split_weights("o")
                    if more:
                        load("o", g + 1)
                    for pair in range(PAIRS):
                        b, h = divmod(pair, G)
                        next_b = 1 - b
                        projects = more or b == 0
                        scores(b, h)
                        if pair:
                            turn_probabilities((h - 1) % G)
                        if h < G - 1:
                            turn_q(b, h + 1)
                        exponentials(h)
                        early = pair in (1, 2)
                        if early:
                            for t in PROJECT[h]:
                                project(next_b, t)
                        if pair in OUT:
                            project_out(*OUT[pair])
                        probabilities(h)
                        if pair:
                            weigh_values(*divmod(pair - 1, G))
                        if b == B - 1:
                            evac.wait(pool)
                            settle(pool)
                            bias_ready[h] = bias_done.mark(pool.tensor_scalar(bias[:, h, :], bias[:, h, :], 0.5, None, ALU.mult))
                        if projects and not early:
                            for t in PROJECT[h]:
                                project(next_b, t)
                        if projects and h == G - 2:
                            norm_rows(next_b)
                        if h == G - 1 and projects:
                            if b == 0:
                                turn_k(next_b)
                                turn_q(next_b, 0)
                                if more:
                                    split_weights("qkv")
                    turn_probabilities(G - 1)
                    project_out(B - 1, 0, (2, 3))
                    weigh_values(B - 1, G - 1)
                    if more:
                        turn_k(0)
                        turn_q(0, 0)
                    project_out(B - 1, 1, tuple(range(TB)), ATT_SPARE if more else 0)

                fresh_memory(sp)
                fresh_memory(act)
                fresh_memory(pool)
                load("qkv", 0)
                load("o", 0)
                bias_done.mark(pool.iota(distance[:, :], pattern=[[1, S]], base=-(S - P), channel_multiplier=-1))
                bias_done.wait(pool)
                for h in range(G):
                    bias_done.mark(pool.tensor_scalar(bias[:, h, :], distance[:, :], float(np.float32(SLOPE0 ** (h + 1))), None, ALU.mult))
                bias_done.wait(pool)
                for h in range(G):
                    bias_ready[h] = bias_done.mark(pool.affine_select(
                        out=bias[:, h, :], in_=bias[:, h, :], compare_op=ALU.is_ge, fill=MASKED, base=S - P,
                        pattern=[[-1, S]], channel_multiplier=1))
                split_weights("qkv")
                layer_norm()
                for t in range(TB):
                    project(0, t)
                norm_rows(0)
                turn_k(0)
                turn_q(0, 0, TB + ATT_SPARE)
                with loop("att", HKV - 1) as g:
                    group(g, True)
                group(HKV - 1, False)

        ffn("_1")
        attention()
        ffn("_2")
        out_rows = out.rearrange("b (t p) c -> p (b t) c", p=P)
        evac.wait(sp)
        x_out.mark(sp.dma_start(out_rows, xr[:, :, :]), 16)
        x_out.wait(sp)


def kernel(**inputs):
    import concourse.bacc as bacc
    from concourse.bass_utils import run_bass_kernel_spmd

    a = {k.removeprefix("L0_"): np.asarray(v) for k, v in inputs.items()}

    def rows_by_chunk(wt, chunk):
        k = wt.shape[0] // P
        return wt.reshape(k, P, -1, chunk).transpose(2, 1, 0, 3).reshape(-1, P, k * chunk)

    gate, up = (rows_by_chunk(a[f"ffn_{n}_w"].T, P).reshape(STEPS, CH, P, KC * P) for n in ("gate", "up"))
    down = a["ffn_down_w"].T.reshape(STEPS, CH, P, DM)
    ffn_w = np.concatenate([t for c in range(CH) for t in (gate[:, c], up[:, c])] + [down[:, c] for c in range(CH)], axis=2)
    su_g, su_u = (a[f"ffn_{n}_su"].T.reshape(R, STEPS, CH, P) for n in ("gate", "up"))
    sv_d = a["ffn_down_sv"].reshape(R, STEPS, CH * P)
    ffn_fac = np.stack([np.concatenate([su_g[:, :, c], su_u[:, :, c]], axis=2) for c in range(CH)] + [sv_d], axis=0)
    ffn_fac = ffn_fac.transpose(2, 0, 1, 3)
    ffn_fix = np.concatenate([a["ffn_gate_sv"], a["ffn_up_sv"], a["ffn_down_su"].T], axis=1)
    q = a["attn_Wq"].T.reshape(KC, P, HKV, QW)
    k, v = (a[f"attn_{n}"].T.reshape(KC, P, HKV, HD) for n in ("Wk", "Wv"))
    w_qkv = np.concatenate([q, k, v], axis=3).transpose(2, 1, 0, 3).reshape(HKV, P, KC * QKVW)
    w_o = a["attn_Wo"].T.reshape(HKV, G, P, DM).transpose(0, 2, 1, 3).reshape(HKV, P, G * DM)
    norm_w = np.stack([a["attn_q_norm_w"], a["attn_k_norm_w"]], axis=1)
    arrays = {"x": a["attn_x"], "ffn_w": ffn_w, "ffn_fac": ffn_fac, "ffn_fix": ffn_fix,
              "w_qkv": w_qkv, "w_o": w_o, "norm_w": norm_w}
    arrays = {name: np.ascontiguousarray(v) for name, v in arrays.items()}

    nc = bacc.Bacc("TRN2", target_bir_lowering=False, num_devices=1)
    args = [nc.dram_tensor(name, v.shape, mybir.dt.from_np(v.dtype), kind="ExternalInput").ap() for name, v in arrays.items()]
    args.append(nc.dram_tensor("y", (B, S, DM), F32, kind="ExternalOutput").ap())
    build(nc, *args)
    return run_bass_kernel_spmd(nc, [arrays], core_ids=[0]).results[0]["y"]
```

```python
from contextlib import ExitStack, contextmanager

import numpy as np

import concourse.bass as bass
from concourse import mybir

F32, F32R, I32 = mybir.dt.float32, mybir.dt.float32r, mybir.dt.int32
ALU = mybir.AluOpType
ACT = mybir.ActivationFunctionType
AX = mybir.AxisListType

P = 128
BANKS = 8
B, S, DM = 2, 512, 512
KC = DM // P
TB = S // P
H, HKV, HD = 32, 8, 128
G = H // HKV
QW = G * HD
QKW = QW + HD
QKVW = QKW + HD
FI = 1792
R = 4
CH = 2
STEPS = FI // P // CH
LN_EPS, RMS_EPS = 1e-5, 1e-6
MASKED = -1e30
NEWTONS = 3
ROOT_MAGIC = 1597463007.0
SLOPE0 = 2 ** -(2 ** -(np.log2(H) - 3))
assert abs(SLOPE0 ** G - 0.5) < 1e-12


class Mark:

    def __init__(self, count):
        self.count = count


class Tally:

    def __init__(self, sem, per):
        self.sem, self.per = sem, per
        self.count, self.loop, self.made = 0, None, []

    def mark(self, instruction, by=1, spare=0):
        instruction.then_inc(self.sem, by + spare)
        m = Mark(self.count + by)
        self.count += by + spare
        if self.loop:
            self.made.append(m)
        return m

    def wait(self, engine, until=None):
        count = self.count if until is None else until.count if isinstance(until, Mark) else until
        if self.loop:
            name, i = self.loop
            if name in self.per:
                count = i * self.per[name] + count
        elif count <= 0:
            return
        engine.wait_ge(self.sem, count)


def build(nc, x, ffn_w, ffn_fac, ffn_fix, w_qkv, w_o, norm_w, out):
    with ExitStack() as ctx:
        def sb(name, shape, dt=F32, stack=ctx):
            return stack.enter_context(nc.sbuf_tensor(name, [P, *shape], dt))

        tallies = []

        def tally(name, **per):
            t = Tally(ctx.enter_context(nc.semaphore(name)), per)
            tallies.append(t)
            return t

        @contextmanager
        def loop(name, n):
            with nc.Fori(0, n) as i:
                starts = [t.count for t in tallies]
                for t in tallies:
                    t.loop, t.made = (name, i), []
                yield i
                for t, start in zip(tallies, starts):
                    per = t.count - start
                    assert per == t.per.get(name, 0), (name, t.sem.name, per)
                    t.count += (n - 1) * per
                    t.loop = None
                    for m in t.made:
                        m.count += (n - 1) * per

        pe, act, dve, pool, sp = nc.tensor, nc.scalar, nc.vector, nc.gpsimd, nc.sync
        banks = [ctx.enter_context(nc.psum_tensor(f"bank{i}", [P, 512], F32)) for i in range(BANKS)]

        PAIRS = B * G
        FFN_SPLITS = 2 * (2 * CH - CH + 1)
        FFN_RESULTS = 2 * CH * B + TB * B + FFN_SPLITS
        FFN_SPARE = -FFN_RESULTS % BANKS
        PROB_RESULTS = 3
        ATT_RESULTS = B * (2 * TB + 1) + PAIRS * (1 + TB + PROB_RESULTS + 1) + PAIRS // 2 * TB
        ATT_SPARE = -ATT_RESULTS % BANKS
        KINDS = ("gu0", "gu1", "down")

        full = tally("full", ffn=FFN_RESULTS + FFN_SPARE, att=ATT_RESULTS + ATT_SPARE)
        evac = tally("evac", ffn=FFN_RESULTS + FFN_SPARE, att=ATT_RESULTS + ATT_SPARE)
        hi_done = tally("hi_done", ffn=2 * CH * B, att=PAIRS * (PROB_RESULTS + 2) + B + B * TB * 3)
        gated = tally("gated", ffn=CH * B)
        exp_done = tally("exp_done", att=PAIRS)
        top_done = tally("top_done", att=PAIRS)
        prob_done = tally("prob_done", att=PAIRS)
        root_done = tally("root_done", att=B)
        rows_done = tally("rows_done", att=B * (G + 1))
        bias_done = tally("bias_done", att=G)
        own = tally("own", att=PAIRS + B * (TB + 1 + 3 * NEWTONS))
        w_hi = tally("w_hi", ffn=FFN_SPLITS, att=KC + G)
        w_lo = tally("w_lo", ffn=FFN_SPLITS, att=KC + G)
        fac_hi = tally("fac_hi", ffn=len(KINDS))
        fac_done = tally("fac_done", ffn=len(KINDS))
        w_in = {k: tally(f"w_in_{k}", ffn=16) for k in KINDS} | {k: tally(f"w_in_{k}", att=16) for k in ("qkv", "o")}
        fac_in = {k: tally(f"fac_in_{k}", ffn=16 * 4) for k in KINDS}
        x_in = [tally(f"x_in{t}") for t in range(B * TB)]
        norm_in = tally("norm_in")
        fix_in = tally("fix_in")
        ready = tally("ready")
        rows_set = tally("rows_set")
        xn_done = tally("xn_done")
        x_out = tally("x_out")

        passed = ctx.enter_context(nc.semaphore("passed"))

        def settle(engine):
            engine.sem_inc(passed, 1)

        def next_bank(operand=Mark(0)):
            evac.wait(pe, max(full.count + 1, operand.count))
            return banks[full.count % BANKS]

        xr = sb("x_rows", [B * TB, DM])
        xnT_hi = sb("xnT_hi", [KC, B * S], F32R)
        xnT_lo = sb("xnT_lo", [KC, B * S], F32R)
        row_room = sb("row_room", [B, TB * (G + 1) * HD])
        xn = row_room[:, :, 0:TB * DM].rearrange("p b (t c) -> p b t c", t=TB)
        rows = row_room[:, :, :].rearrange("p b (t h d) -> p b t h d", t=TB, h=G + 1)
        ident = sb("ident", [P])
        wcol = sb("wcol", [2])
        wkcol = sb("wkcol", [1])
        stats = sb("stats", [B * TB, 6])
        mv = sb("mv", [B * TB, 2])
        ROOTS = TB * (G + 1)
        root_m, root_y, root_a, root_b = (sb(f"root_{n}", [ROOTS]) for n in "myab")
        bias = sb("bias", [G, S])
        COLS = dict(gu0=2 * DM, gu1=2 * DM, down=CH * DM)
        START = dict(gu0=0, gu1=2 * DM, down=4 * DM)
        FFN_W = 4 * DM + CH * DM
        assert FFN_W == KC * QKVW and G * DM <= FFN_W
        fac_raw = {k: sb(f"fac_raw_{k}", [2 * P]) for k in KINDS}
        fac = {k: sb(f"fac_{k}", [2 * P], F32R) for k in KINDS}
        fix = sb("fix", [3 * DM], F32R)

        def weight_room(name, stack=ctx):
            return (sb(f"raw_{name}", [FFN_W], F32, stack), sb(f"w_h_{name}", [FFN_W], F32R, stack),
                    sb(f"w_l_{name}", [FFN_W], F32R, stack))

        late_room = weight_room("late")

        own_last = [None]

        def own_step(instruction):
            own_last[0] = own.mark(instruction)

        def own_wait():
            own.wait(dve, own_last[0])

        def inverse_root(mean_square, eps, n, scale=1.0):
            m, y, a, b = (t[:, 0:n] for t in (root_m, root_y, root_a, root_b))
            own_wait()
            yield own_step(dve.tensor_scalar(m, mean_square, scale, eps, ALU.mult, ALU.add))
            own_wait()
            yield own_step(dve.tensor_scalar(y.bitcast(I32), m.bitcast(I32), -0.5, ROOT_MAGIC, ALU.mult, ALU.add))
            for newton in range(NEWTONS):
                own_wait()
                yield own_step(dve.scalar_tensor_tensor(a, y, -0.5, y, ALU.mult, ALU.mult))
                own_wait()
                yield own_step(dve.tensor_tensor(b, a, m, ALU.mult))
                own_wait()
                last = dve.scalar_tensor_tensor(y, b, 1.5, y, ALU.add, ALU.mult)
                yield own_step(last) if newton < NEWTONS - 1 else last

        def matmul3(bank, left, right, first, last):
            (lh, ll), (rh, rl) = left, right
            pe.matmul(bank, lh, rh, start=first, stop=False)
            pe.matmul(bank, lh, rl, start=False, stop=False)
            return pe.matmul(bank, ll, rh, start=False, stop=last)

        def split_result(n, src, hi, lo, scale=None, spare=0):
            full.wait(act, n)
            if scale is None:
                hi_done.mark(act.copy(hi, src))
            else:
                hi_done.mark(act.activation(hi, src, ACT.Copy, scale=scale))
            hi_done.wait(dve)
            if scale is None:
                last = dve.tensor_tensor(lo, src, hi.bitcast(F32), ALU.subtract)
            else:
                last = dve.scalar_tensor_tensor(lo, src, scale, hi.bitcast(F32), ALU.mult, ALU.subtract)
            return evac.mark(last, spare=spare)

        row_read, xn_ready = {}, {}

        def statistics(t):
            evac.wait(dve)
            own_step(dve.bn_stats(stats[:, t, :], xr[:, t, :]))

        def normalize(b):
            blocks = slice(b * TB, (b + 1) * TB)
            own_wait()
            for t in range(B * TB)[blocks]:
                last = dve.bn_aggr(mv[:, t, :], stats[:, t, :])
                yield
            own_step(last)
            rows_done.wait(dve)
            for last in inverse_root(mv[:, blocks, 1], LN_EPS, TB):
                yield
            own_step(last)
            own_wait()
            if b in row_read:
                full.wait(dve, row_read[b])
            for t in range(TB):
                xn_done.mark(dve.tensor_scalar(xn[:, b, t, :], xr[:, b * TB + t, :], mv[:, b * TB + t, 0:1], root_y[:, t:t + 1],
                                               ALU.subtract, ALU.mult))
                yield

        def finish(steps):
            for _ in steps:
                pass

        def turn_normed(b, between=iter(())):
            for t in range(TB):
                xn_done.wait(pe, Mark(xn_done.count - TB + t + 1))
                bank = next_bank()
                for k in range(KC):
                    last = pe.transpose(bank[:, k * P:(k + 1) * P], xn[:, b, t, k * P:(k + 1) * P], ident[:, :])
                row_read[b] = full.mark(last)
                cols = slice(b * S + t * P, b * S + (t + 1) * P)
                xn_ready[b] = split_result(row_read[b], bank[:, :].rearrange("p (k c) -> p k c", k=KC),
                                           xnT_hi[:, :, cols], xnT_lo[:, :, cols])
                for _ in range(6):
                    next(between, None)

        lo_rows = sb("lo_rows", [2])
        LEFT, RIGHT = lo_rows[:, 0:1], lo_rows[:, 1:2]
        fac_ready, w_ready = {}, {}

        def split_factor(raw, stack, parts):
            for cols, lo in parts:
                last = act.activation(stack[:, cols], raw[:, cols], ACT.Copy, scale=lo)
            fac_hi.mark(last)
            fac_hi.wait(pool)
            return fac_done.mark(pool.tensor_tensor(stack[:, :], raw[:, :], stack[:, :].bitcast(F32), ALU.subtract))

        def stack_factors(kind):
            fac_in[kind].wait(act)
            full.wait(act)
            fac_ready[kind] = split_factor(fac_raw[kind], fac[kind], [(slice(0, 2 * P), LEFT if kind == "down" else RIGHT)])

        def load_ffn(room, kind, step):
            at = slice(step, step + 1) if isinstance(step, int) else bass.ds(step, 1)
            w_lo.wait(sp)
            settle(sp)
            fac_done.wait(sp)
            settle(sp)
            cols = slice(START[kind], START[kind] + COLS[kind])
            for g in range(4):
                fac_in[kind].mark(sp.dma_start(fac_raw[kind][32 * g:32 * g + R, :],
                                               ffn_fac[at][:, KINDS.index(kind)].rearrange("s r c -> r (s c)")), 16)
            w_in[kind].mark(sp.dma_start(room[0][:, cols], ffn_w[at][:, :, cols].rearrange("s p c -> p (s c)")), 16)

        def scale_weights(room, kind, spare=0):
            raw, w_h, w_l = room
            fac_done.wait(pe, fac_ready[kind])
            for half in range(2):
                bank = next_bank()
                one = slice(half * P, (half + 1) * P)
                if kind == "down":
                    last = pe.matmul(bank[:, :], fac[kind][:, one], fix[:, 2 * DM:3 * DM], start=True, stop=True)
                else:
                    for k in range(KC):
                        at = slice(half * DM + k * P, half * DM + (k + 1) * P)
                        last = pe.matmul(bank[:, k * P:(k + 1) * P], fix[:, at], fac[kind][:, one],
                                         start=True, stop=True, skip_group_check=True)
                n = full.mark(last, spare=spare * half)
                cols = slice(START[kind] + half * DM, START[kind] + (half + 1) * DM)
                w_in[kind].wait(dve)
                full.wait(dve, n)
                evac.mark(dve.tensor_tensor(raw[:, cols], bank[:, :], raw[:, cols], ALU.mult), spare=spare * half)
                evac.wait(act)
                w_hi.mark(act.copy(w_h[:, cols], raw[:, cols]))
                w_hi.wait(pool)
                w_ready[kind] = w_lo.mark(pool.tensor_tensor(w_l[:, cols], raw[:, cols], w_h[:, cols].bitcast(F32),
                                                             ALU.subtract))

        def ffn(tag, room, prepare, finished, last_part):
            with ExitStack() as part_memory:
                def psb(name, shape, dt=F32):
                    return sb(name + tag, shape, dt, part_memory)

                silu = psb("silu", [CH, S])
                d = psb("d", [CH, S])
                d_hi = psb("d_hi", [CH, B, S], F32R)
                d_lo = psb("d_lo", [CH, B, S], F32R)
                w_h, w_l = room[1:]
                d_ready = {}

                def gate_up(c, b):
                    kind = f"gu{c}"
                    w_lo.wait(pe, w_ready[kind])
                    results = []
                    for half in range(2):
                        bank = next_bank(xn_ready[b])
                        for k in range(KC):
                            w = START[kind] + half * DM + k * P
                            w = slice(w, w + P)
                            tokens = slice(b * S, (b + 1) * S)
                            last = matmul3(bank[:, :], (w_h[:, w], w_l[:, w]),
                                           (xnT_hi[:, k, tokens], xnT_lo[:, k, tokens]), k == 0, k == KC - 1)
                        results.append((full.mark(last), bank))
                    (n_a, bank_a), (n_b, bank_b) = results
                    full.wait(act, n_a)
                    hi_done.mark(act.activation(silu[:, c, :], bank_a[:, :], ACT.Silu))
                    hi_done.wait(dve)
                    full.wait(dve, n_b)
                    gated.mark(dve.tensor_tensor(d[:, c, :], bank_b[:, :], silu[:, c, :], ALU.mult))
                    gated.wait(act)
                    hi_done.mark(act.copy(d_hi[:, c, b, :], d[:, c, :]))
                    hi_done.wait(dve)
                    d_ready[b] = evac.mark(dve.tensor_tensor(d_lo[:, c, b, :], d[:, c, :], d_hi[:, c, b, :].bitcast(F32),
                                                             ALU.subtract), 2)

                def down(b, ends):
                    w_lo.wait(pe, w_ready["down"])
                    for t in range(TB):
                        bank = next_bank(d_ready[b])
                        tokens = slice(t * P, (t + 1) * P)
                        for c in range(CH):
                            w = START["down"] + c * DM
                            w = slice(w, w + DM)
                            last = matmul3(bank[:, :], (d_hi[:, c, b, tokens], d_lo[:, c, b, tokens]),
                                           (w_h[:, w], w_l[:, w]), c == 0, c == CH - 1)
                        full.wait(dve, full.mark(last))
                        row = xr[:, b * TB + t, :]
                        evac.mark(dve.scalar_tensor_tensor(row, bank[:, :], 0.5, row, ALU.mult, ALU.add))
                        if ends:
                            finished(b * TB + t)

                def step(i, more):
                    if more:
                        for kind in KINDS:
                            load_ffn(room, kind, i + 1)
                    gate_up(1, 0)
                    if more:
                        stack_factors("gu0")
                    gate_up(0, 1)
                    if more:
                        scale_weights(room, "gu0")
                    if last_part and not more:
                        gate_up(1, 1)
                        down(0, True)
                        down(1, True)
                        return
                    down(0, not more)
                    if more:
                        stack_factors("gu1")
                    else:
                        finish(normalize(0))
                    gate_up(1, 1)
                    if more:
                        scale_weights(room, "gu1")
                        stack_factors("down")
                        gate_up(0, 0)
                    else:
                        turn_normed(0)
                    down(1, not more)
                    if more:
                        scale_weights(room, "down", FFN_SPARE)

                finish(normalize(1))
                gate_up(0, 0)
                turn_normed(1)
                with loop("ffn", STEPS - 1) as i:
                    step(i, True)
                prepare()
                step(STEPS - 1, False)

        qkv_room, o_room = ([t[:, 0:KC * QKVW].rearrange("p (k c) -> p k c", k=KC) for t in late_room],
                            [late_room[0][:, 0:G * DM].rearrange("p (k c) -> p k c", k=G)])
        bias_ready = {}

        def load_attention(kind, step):
            at = slice(step, step + 1) if isinstance(step, int) else bass.ds(step, 1)
            w_lo.wait(sp)
            settle(sp)
            src, chunks = (w_qkv, KC * QKVW) if kind == "qkv" else (w_o, G * DM)
            w_in[kind].mark(sp.dma_start(late_room[0][:, 0:chunks], src[at].rearrange("s p c -> p (s c)")), 16)

        def split_weights(kind, raw, hi, lo):
            w_in[kind].wait(act)
            full.wait(act)
            for k in range(KC if kind == "qkv" else G):
                w_hi.mark(act.copy(hi[:, k, :], raw[:, k, :]))
                w_hi.wait(pool)
                w_ready[kind] = w_lo.mark(pool.tensor_tensor(lo[:, k, :], raw[:, k, :], hi[:, k, :].bitcast(F32),
                                                             ALU.subtract))

        def first_biases(distance):
            bias_done.mark(pool.iota(distance[:, :], pattern=[[1, S]], base=-(S - P), channel_multiplier=-1))
            bias_done.wait(pool)
            for h in range(G):
                bias_done.mark(pool.tensor_scalar(bias[:, h, :], distance[:, :], float(np.float32(SLOPE0 ** (h + 1))), None, ALU.mult))
            bias_done.wait(pool)
            for h in range(G):
                bias_ready[h] = bias_done.mark(pool.affine_select(
                    out=bias[:, h, :], in_=bias[:, h, :], compare_op=ALU.is_ge, fill=MASKED, base=S - P,
                    pattern=[[-1, S]], channel_multiplier=1))

        def attention():
            with ExitStack() as part_memory:
                def psb(name, shape, dt=F32):
                    return sb(name, shape, dt, part_memory)

                _, qkv_h, qkv_l = qkv_room
                o_h, o_l = psb("o_h", [G, DM], F32R), psb("o_l", [G, DM], F32R)
                o_all = (o_room[0], o_h, o_l)
                square = psb("square", [G + 1, HD])
                sums = psb("sums", [TB, G + 1])
                v_h, v_l = psb("v_h", [B, TB, HD], F32R), psb("v_l", [B, TB, HD], F32R)
                kT_h, kT_l = psb("kT_h", [B, S], F32R), psb("kT_l", [B, S], F32R)
                qT_h, qT_l = psb("qT_h", [2, S], F32R), psb("qT_l", [2, S], F32R)
                OFF = [P * i * (i + 1) // 2 for i in range(TB + 1)]
                prob = psb("prob", [2, OFF[TB]])
                probT_h, probT_l = psb("probT_h", [OFF[TB]], F32R), psb("probT_l", [OFF[TB]], F32R)
                oT_h, oT_l = psb("oT_h", [2, 2, S], F32R), psb("oT_l", [2, 2, S], F32R)
                top, neg_top, total, inverse = (psb(n, [2, TB]) for n in ("top", "neg_top", "total", "inverse"))
                TURNS = [[(0, 0)], [(1, 0), (3, 3 * P)], [(2, 0)]]
                probT_at = {j: S * n + at for n, turn in enumerate(TURNS) for j, at in turn}
                assert len(TURNS) == PROB_RESULTS and TB == 4
                rows_ready, oT_ready, row_summed, q_ready, probT_ready = {}, {}, {}, [None], [None]

                def project(b, t):
                    w_lo.wait(pe, w_ready["qkv"])
                    results = []
                    tokens = slice(b * S + t * P, b * S + (t + 1) * P)
                    for cols in (slice(0, QW), slice(QW, QKVW)):
                        bank = next_bank(xn_ready[b])
                        for k in range(KC):
                            last = matmul3(bank[:, 0:cols.stop - cols.start], (xnT_hi[:, k, tokens], xnT_lo[:, k, tokens]),
                                           (qkv_h[:, k, cols], qkv_l[:, k, cols]), k == 0, k == KC - 1)
                        results.append((full.mark(last), bank))
                    (n_q, bank_q), (n_kv, bank_kv) = results
                    q, k = rows[:, b, t, 0:G, :], rows[:, b, t, G, :]
                    bank_q = bank_q[:, :].rearrange("p (h d) -> p h d", h=G)
                    full.wait(act, n_q)
                    q_copied = hi_done.mark(act.copy(q, bank_q))
                    full.wait(act, n_kv)
                    hi_done.mark(act.copy(k, bank_kv[:, 0:HD]))
                    hi_done.mark(act.copy(v_h[:, b, t, :], bank_kv[:, HD:2 * HD]))
                    own_wait()
                    hi_done.wait(dve, q_copied)
                    evac.mark(dve.tensor_tensor(square[:, 0:G, :], bank_q, q, ALU.mult))
                    hi_done.wait(dve)
                    dve.tensor_tensor(v_l[:, b, t, :], bank_kv[:, HD:2 * HD], v_h[:, b, t, :].bitcast(F32), ALU.subtract)
                    evac.mark(dve.tensor_tensor(square[:, G, :], bank_kv[:, 0:HD], k, ALU.mult))
                    evac.wait(dve)
                    own_step(dve.tensor_reduce(sums[:, t, :], square[:, :, :], AX.X, ALU.add))

                def row_roots():
                    rows_done.wait(dve)
                    for last in inverse_root(sums[:, :, :].rearrange("p t h -> p (t h)"), RMS_EPS, ROOTS, 1.0 / HD):
                        yield
                    root_done.mark(last)

                def norm_rows(b):
                    root_done.wait(pool)
                    root = root_y[:, :].rearrange("p (t h) -> p t h", h=G + 1)
                    for head in (G, *range(G)):
                        by = root[:, :, head].unsqueeze(2).to_broadcast([P, TB, HD])
                        rows_ready[head] = rows_done.mark(pool.tensor_tensor(rows[:, b, :, head], rows[:, b, :, head], by, ALU.mult))

                def turn_rows(b, head, hi, lo, weight, spare=0):
                    rows_done.wait(pe, rows_ready[head])
                    bank = next_bank()
                    for t in range(TB):
                        last = pe.transpose(bank[:, t * P:(t + 1) * P], rows[:, b, t, head, :], ident[:, :])
                    row_read[b] = full.mark(last, spare=spare)
                    return split_result(row_read[b], bank[:, :], hi, lo, weight, spare)

                def turn_k(b):
                    turn_rows(b, G, kT_h[:, b, :], kT_l[:, b, :], wkcol[:, 0:1])

                def turn_q(b, h, spare=0):
                    q_ready[0] = turn_rows(b, h, qT_h[:, h % 2, :], qT_l[:, h % 2, :], wcol[:, 0:1], spare)

                def scores(b, h, between=iter(())):
                    s = h % 2
                    for i in range(TB):
                        bank = next_bank(q_ready[0])
                        n_keys = (i + 1) * P
                        q = slice(i * P, (i + 1) * P)
                        last = matmul3(bank[:, 0:n_keys], (qT_h[:, s, q], qT_l[:, s, q]),
                                       (kT_h[:, b, 0:n_keys], kT_l[:, b, 0:n_keys]), True, True)
                        full.wait(dve, full.mark(last))
                        bias_done.wait(dve, bias_ready[h])
                        settle(dve)
                        evac.mark(dve.tensor_tensor_reduce(
                            prob[:, s, OFF[i]:OFF[i + 1]], bank[:, 0:n_keys], bias[:, h, S - n_keys:S], 1.0, MASKED,
                            ALU.add, ALU.max, top[:, s, i:i + 1]))
                        for _ in range(3):
                            next(between, None)
                    evac.wait(dve)
                    top_done.mark(dve.tensor_scalar(neg_top[:, s, :], top[:, s, :], -1.0, None, ALU.mult))

                def exponentials(h):
                    s = h % 2
                    top_done.wait(act)
                    for i in range(TB):
                        p = prob[:, s, OFF[i]:OFF[i + 1]]
                        last = act.activation(p, p, ACT.Exp, bias=neg_top[:, s, i:i + 1], accum_out=total[:, s, i:i + 1])
                    exp_done.mark(last)

                def probabilities(h):
                    s = h % 2
                    exp_done.wait(dve)
                    own_step(dve.reciprocal(inverse[:, s, :], total[:, s, :]))
                    own_wait()
                    for i in range(TB):
                        p = prob[:, s, OFF[i]:OFF[i + 1]]
                        last = dve.tensor_scalar(p, p, inverse[:, s, i:i + 1], None, ALU.mult)
                    prob_done.mark(last)

                def turn_probabilities(h):
                    s = h % 2
                    prob_done.wait(pe)
                    for n, turn in enumerate(TURNS):
                        bank = next_bank()
                        for j, at in turn:
                            for i in range(j, TB):
                                here = at + (i - j) * P
                                last = pe.transpose(bank[:, here:here + P], prob[:, s, OFF[i] + j * P:OFF[i] + (j + 1) * P], ident[:, :])
                        width = here + P
                        here = slice(n * S, n * S + width)
                        probT_ready[0] = split_result(full.mark(last), bank[:, 0:width], probT_h[:, here], probT_l[:, here])

                def weigh_values(b, h):
                    bank = next_bank(probT_ready[0])
                    for j in range(TB):
                        width = S - j * P
                        here = slice(probT_at[j], probT_at[j] + width)
                        last = matmul3(bank[:, j * P:S], (v_h[:, b, j, :], v_l[:, b, j, :]),
                                       (probT_h[:, here], probT_l[:, here]), j == 0, j == TB - 1)
                    half = h // 2
                    oT_ready[half] = split_result(full.mark(last), bank[:, :], oT_h[:, half, h % 2, :], oT_l[:, half, h % 2, :])

                def project_out(b, half, blocks, spare=0, ends=False):
                    w_lo.wait(pe, w_ready["o"])
                    for t in blocks:
                        bank = next_bank(oT_ready[half])
                        tokens = slice(t * P, (t + 1) * P)
                        for n in range(2):
                            h = 2 * half + n
                            last = matmul3(bank[:, :], (oT_h[:, half, n, tokens], oT_l[:, half, n, tokens]),
                                           (o_h[:, h, :], o_l[:, h, :]), n == 0, n == 1)
                        spared = spare if t == blocks[-1] else 0
                        if (b, half, t) == (B - 1, 1, TB - 1):
                            evac.wait(dve, row_summed[t])
                        full.wait(dve, full.mark(last, spare=spared))
                        row = xr[:, b * TB + t, :]
                        row_summed[t] = evac.mark(dve.tensor_tensor(row, bank[:, :], row, ALU.add), spare=spared)
                        if ends:
                            statistics(b * TB + t)

                RESULTS_AFTER_Q = 1 + 1 + 1 + 1 + TB
                PROJECT = [(0, 1), (2,), (3,), ()]
                OUT = {3: (0, 0, (0,)), 4: (0, 0, (2, 3)), 5: (0, 1, (0, 1)), 6: (0, 1, (2, 3)), 7: (1, 0, (0, 1))}
                OUT_LATE = {3: (0, 0, (1,))}

                def group(g, more):
                    split_weights("o", *o_all)
                    if more:
                        load_attention("qkv", g + 1)
                    else:
                        for kind in KINDS:
                            load_ffn(late_room, kind, 0)
                    roots = iter(())
                    spare = iter([1] * ATT_SPARE if more else [])
                    for pair in range(PAIRS):
                        b, h = divmod(pair, G)
                        next_b = 1 - b
                        projects = more or b == 0
                        early = h in (1, 2) and projects
                        if pair == PAIRS - 1 and not more:
                            roots = normalize(0)
                        scores(b, h, roots)
                        if h == G - 1 and projects:
                            finish(roots)
                            norm_rows(next_b)
                        if b == B - 1 and more:
                            for head in {G - 1: (G - 2, G - 1)}.get(h, (h,) if h < G - 2 else ()):
                                evac.wait(pool)
                                settle(pool)
                                bias_ready[head] = bias_done.mark(pool.tensor_scalar(bias[:, head, :], bias[:, head, :], 0.5, None, ALU.mult))
                        if pair:
                            turn_probabilities((h - 1) % G)
                        if h < G - 1:
                            turn_q(b, h + 1)
                        exponentials(h)
                        if early:
                            probabilities(h)
                            for t in PROJECT[h]:
                                project(next_b, t)
                        if pair in OUT:
                            out_b, half, blocks = OUT[pair]
                            project_out(out_b, half, blocks, next(spare, 0), not more and (out_b, half) == (0, 1))
                        if pair == G - 1:
                            turn_k(next_b)
                            turn_q(next_b, 0)
                        if not early:
                            probabilities(h)
                        if h == G - 2 and projects:
                            roots = row_roots()
                            for _ in range(6):
                                next(roots)
                        if pair:
                            weigh_values(*divmod(pair - 1, G))
                        if pair in OUT_LATE:
                            project_out(*OUT_LATE[pair])
                        if projects and not early:
                            for t in PROJECT[h]:
                                project(next_b, t)
                        if pair == G - 1 and more:
                            split_weights("qkv", *qkv_room)
                            load_attention("o", g + 1)
                        if not more and G - 1 <= pair < G - 1 + len(KINDS):
                            stack_factors(KINDS[pair - G + 1])
                        if not more and G <= pair < G + len(KINDS):
                            scale_weights(late_room, KINDS[pair - G])
                    finish(roots)
                    turn_probabilities(G - 1)
                    if more:
                        turn_k(0)
                        turn_q(0, 0)
                    project_out(B - 1, 0, (2,), next(spare, 0))
                    weigh_values(B - 1, G - 1)
                    if not more:
                        turn_normed(0)
                    project_out(B - 1, 0, (3,))
                    project_out(B - 1, 1, tuple(range(TB)), ends=not more)
                    assert not list(spare)

                bias_done.wait(act)
                bias_done.wait(dve)
                finish(normalize(1))
                for t in range(TB):
                    project(0, t)
                roots = row_roots()
                turn_normed(1, roots)
                finish(roots)
                norm_rows(0)
                turn_k(0)
                turn_q(0, 0, RESULTS_AFTER_Q)
                ahead = evac.count - q_ready[0].count
                with loop("att", HKV - 1) as g:
                    group(g, True)
                    assert evac.count - q_ready[0].count == ahead
                group(HKV - 1, False)

        x_rows = x.rearrange("b (t p) c -> (b t) p c", p=P)
        out_rows = out.rearrange("b (t p) c -> (b t) p c", p=P)
        with ExitStack() as early_memory:
            early_room = weight_room("early", early_memory)
            fix_raw = sb("fix_raw", [3 * DM], F32, early_memory)
            distance = sb("distance", [S], I32, early_memory)

            for t in range(TB):
                x_in[t].mark(sp.dma_start(xr[:, t, :], x_rows[t]), 16)
            rows_set.mark(dve.memset(fix_raw[:, :], 0.0))
            for t in fac_raw.values():
                ready.mark(pool.memset(t[:, :], 0.0))
            for start, left, right in ((0, 0, 0), (32, 0, 1), (64, 1, 0), (96, 1, 1)):
                for column, value in enumerate((left, right)):
                    rows_set.mark(dve.memset(lo_rows[start:start + 32, column:column + 1], float(value)))
            ready.wait(sp)
            rows_set.wait(sp)
            load_ffn(early_room, "gu0", 0)
            for g in range(4):
                fix_in.mark(sp.dma_start(fix_raw[32 * g:32 * g + R, :], ffn_fix), 16)
            for t in range(TB, B * TB):
                x_in[t].mark(sp.dma_start(xr[:, t, :], x_rows[t]), 16)
            load_ffn(early_room, "gu1", 0)
            load_ffn(early_room, "down", 0)
            norm_in.mark(sp.dma_start(wcol[:, :], norm_w), 16)
            load_attention("qkv", 0)
            dve.sem_inc(evac.sem, BANKS)
            evac.count = BANKS
            ready.mark(pool.memset(ident[:, :], 0.0))
            ready.wait(pool)
            ready.mark(pool.affine_select(out=ident[:, :], in_=ident[:, :], compare_op=ALU.not_equal, fill=1.0,
                                          base=0, pattern=[[-1, P]], channel_multiplier=1))
            ready.wait(pe)
            for t in range(TB):
                x_in[t].wait(dve)
                statistics(t)
            finish(normalize(0))
            rows_set.wait(act)
            fix_in.wait(act)
            split_factor(fix_raw, fix, [(slice(0, 2 * DM), LEFT), (slice(2 * DM, 3 * DM), RIGHT)])
            for kind in KINDS:
                stack_factors(kind)
            turn_normed(0)
            for kind in KINDS:
                scale_weights(early_room, kind)
            for t in range(TB, B * TB):
                x_in[t].wait(dve)
                statistics(t)

            def prepare_attention():
                split_weights("qkv", *qkv_room)
                load_attention("o", 0)
                first_biases(distance)

            ffn("_1", early_room, prepare_attention, statistics, False)
        norm_in.wait(dve)
        own_step(dve.tensor_scalar(wkcol[:, :], wcol[:, 1:2], float(HD) ** -0.5, None, ALU.mult))
        attention()

        def store(t):
            evac.wait(sp)
            x_out.mark(sp.dma_start(out_rows[t], xr[:, t, :]), 16)

        ffn("_2", late_room, lambda: None, store, True)
        x_out.wait(sp)


def kernel(**inputs):
    import concourse.bacc as bacc
    from concourse.bass_utils import run_bass_kernel_spmd

    a = {k.removeprefix("L0_"): np.asarray(v) for k, v in inputs.items()}

    def rows_by_chunk(wt, chunk):
        k = wt.shape[0] // P
        return wt.reshape(k, P, -1, chunk).transpose(2, 1, 0, 3).reshape(-1, P, k * chunk)

    gate, up = (rows_by_chunk(a[f"ffn_{n}_w"].T, P).reshape(STEPS, CH, P, KC * P) for n in ("gate", "up"))
    down = a["ffn_down_w"].T.reshape(STEPS, CH, P, DM)
    ffn_w = np.concatenate([t for c in range(CH) for t in (gate[:, c], up[:, c])] + [down[:, c] for c in range(CH)], axis=2)
    su_g, su_u = (a[f"ffn_{n}_su"].T.reshape(R, STEPS, CH, P) for n in ("gate", "up"))
    sv_d = a["ffn_down_sv"].reshape(R, STEPS, CH * P)
    ffn_fac = np.stack([np.concatenate([su_g[:, :, c], su_u[:, :, c]], axis=2) for c in range(CH)] + [sv_d], axis=0)
    ffn_fac = ffn_fac.transpose(2, 0, 1, 3)
    ffn_fix = np.concatenate([a["ffn_gate_sv"], a["ffn_up_sv"], a["ffn_down_su"].T], axis=1)
    q = a["attn_Wq"].T.reshape(KC, P, HKV, QW)
    k, v = (a[f"attn_{n}"].T.reshape(KC, P, HKV, HD) for n in ("Wk", "Wv"))
    w_qkv = np.concatenate([q, k, v], axis=3).transpose(2, 1, 0, 3).reshape(HKV, P, KC * QKVW)
    w_o = a["attn_Wo"].T.reshape(HKV, G, P, DM).transpose(0, 2, 1, 3).reshape(HKV, P, G * DM)
    norm_w = np.stack([a["attn_q_norm_w"], a["attn_k_norm_w"]], axis=1)
    arrays = {"x": a["attn_x"], "ffn_w": ffn_w, "ffn_fac": ffn_fac, "ffn_fix": ffn_fix,
              "w_qkv": w_qkv, "w_o": w_o, "norm_w": norm_w}
    arrays = {name: np.ascontiguousarray(v) for name, v in arrays.items()}

    nc = bacc.Bacc("TRN2", target_bir_lowering=False, num_devices=1)
    args = [nc.dram_tensor(name, v.shape, mybir.dt.from_np(v.dtype), kind="ExternalInput").ap() for name, v in arrays.items()]
    args.append(nc.dram_tensor("y", (B, S, DM), F32, kind="ExternalOutput").ap())
    build(nc, *args)
    return run_bass_kernel_spmd(nc, [arrays], core_ids=[0]).results[0]["y"]
```

```python
from contextlib import ExitStack, contextmanager

import numpy as np

import concourse.bass as bass
from concourse import mybir

F32, F32R, I32 = mybir.dt.float32, mybir.dt.float32r, mybir.dt.int32
ALU = mybir.AluOpType
ACT = mybir.ActivationFunctionType
AX = mybir.AxisListType

P = 128
BANKS = 8
B, S, DM = 2, 512, 512
KC = DM // P
TB = S // P
H, HKV, HD = 32, 8, 128
G = H // HKV
QW = G * HD
QKW = QW + HD
QKVW = QKW + HD
FI = 1792
R = 4
CH = 2
STACK = 2 * 4 * R
STEPS = FI // P // CH
LN_EPS, RMS_EPS = 1e-5, 1e-6
MASKED = -1e30
NEWTONS = 3
ROOT_MAGIC = 1597463007.0
SLOPE0 = 2 ** -(2 ** -(np.log2(H) - 3))
assert abs(SLOPE0 ** G - 0.5) < 1e-12


class Mark:

    def __init__(self, count):
        self.count = count


class Tally:

    def __init__(self, sem, per):
        self.sem, self.per = sem, per
        self.count, self.loop, self.made = 0, None, []

    def mark(self, instruction, by=1, spare=0):
        instruction.then_inc(self.sem, by + spare)
        m = Mark(self.count + by)
        self.count += by + spare
        if self.loop:
            self.made.append(m)
        return m

    def wait(self, engine, until=None):
        count = self.count if until is None else until.count if isinstance(until, Mark) else until
        if self.loop:
            name, i = self.loop
            if name in self.per:
                count = i * self.per[name] + count
        elif count <= 0:
            return
        engine.wait_ge(self.sem, count)


def build(nc, x, ffn_w, ffn_fac, ffn_fix, factor_lo, w_qkv, w_o, norm_w, out):
    with ExitStack() as ctx:
        def sb(name, shape, dt=F32, stack=ctx):
            return stack.enter_context(nc.sbuf_tensor(name, [P, *shape], dt))

        tallies = []

        def tally(name, **per):
            t = Tally(ctx.enter_context(nc.semaphore(name)), per)
            tallies.append(t)
            return t

        @contextmanager
        def loop(name, n):
            with nc.Fori(0, n) as i:
                starts = [t.count for t in tallies]
                for t in tallies:
                    t.loop, t.made = (name, i), []
                yield i
                for t, start in zip(tallies, starts):
                    per = t.count - start
                    assert per == t.per.get(name, 0), (name, t.sem.name, per)
                    t.count += (n - 1) * per
                    t.loop = None
                    for m in t.made:
                        m.count += (n - 1) * per

        pe, act, dve, pool, sp = nc.tensor, nc.scalar, nc.vector, nc.gpsimd, nc.sync
        banks = [ctx.enter_context(nc.psum_tensor(f"bank{i}", [P, 512], F32)) for i in range(BANKS)]

        PAIRS = B * G
        FFN_SPLITS = 2 * (CH + 1)
        FFN_RESULTS = 2 * CH * B + TB * B + FFN_SPLITS
        FFN_SPARE = -FFN_RESULTS % BANKS
        PROB_RESULTS = 3
        ATT_RESULTS = B * (2 * TB + 1) + PAIRS * (1 + TB + PROB_RESULTS + 1) + PAIRS // 2 * TB
        ATT_SPARE = -ATT_RESULTS % BANKS
        KINDS = ("gu0", "gu1", "down")

        full = tally("full", ffn=FFN_RESULTS + FFN_SPARE, att=ATT_RESULTS + ATT_SPARE)
        evac = tally("evac", ffn=FFN_RESULTS + FFN_SPARE, att=ATT_RESULTS + ATT_SPARE)
        hi_done = tally("hi_done", ffn=2 * CH * B, att=PAIRS * (PROB_RESULTS + 2) + B + B * TB * 3)
        gated = tally("gated", ffn=CH * B)
        exp_done = tally("exp_done", att=PAIRS)
        top_done = tally("top_done", att=PAIRS)
        prob_done = tally("prob_done", att=PAIRS)
        root_done = tally("root_done", att=B)
        k_done = tally("k_done", att=B)
        rows_done = tally("rows_done", att=B * G)
        bias_done = tally("bias_done", att=G)
        own = tally("own", att=PAIRS + B * (TB + 1 + 3 * NEWTONS))
        w_hi = tally("w_hi", ffn=FFN_SPLITS, att=KC + G)
        w_lo = tally("w_lo", ffn=FFN_SPLITS, att=KC + G)
        fac_hi = tally("fac_hi", ffn=len(KINDS))
        fac_done = tally("fac_done", ffn=len(KINDS))
        w_in = {k: tally(f"w_in_{k}", ffn=16) for k in KINDS} | {k: tally(f"w_in_{k}", att=16) for k in ("qkv", "o")}
        fac_in = {k: tally(f"fac_in_{k}", ffn=16) for k in KINDS}
        x_in = [tally(f"x_in{t}") for t in range(B * TB)]
        norm_in = tally("norm_in")
        fix_in = tally("fix_in")
        ready = tally("ready")
        xn_done = tally("xn_done")
        x_out = tally("x_out")

        passed = ctx.enter_context(nc.semaphore("passed"))

        def settle(engine):
            engine.sem_inc(passed, 1)

        def next_bank(operand=Mark(0)):
            evac.wait(pe, max(full.count + 1, operand.count))
            return banks[full.count % BANKS]

        xr = sb("x_rows", [B * TB, DM])
        xnT_hi = sb("xnT_hi", [KC, B * S], F32R)
        xnT_lo = sb("xnT_lo", [KC, B * S], F32R)
        row_room = sb("row_room", [B, TB * (G + 1) * HD])
        xn = row_room[:, :, 0:TB * DM].rearrange("p b (t c) -> p b t c", t=TB)
        rows = row_room[:, :, :].rearrange("p b (t h d) -> p b t h d", t=TB, h=G + 1)
        ident = sb("ident", [P])
        wcol = sb("wcol", [2])
        wkcol = sb("wkcol", [1])
        stats = sb("stats", [B * TB, 6])
        mv = sb("mv", [B * TB, 2])
        ROOTS = TB * (G + 1)
        root_m, root_y, root_a, root_b = (sb(f"root_{n}", [ROOTS]) for n in "myab")
        bias = sb("bias", [G, S])
        COLS = dict(gu0=2 * DM, gu1=2 * DM, down=CH * DM)
        START = dict(gu0=0, gu1=2 * DM, down=4 * DM)
        FFN_W = 4 * DM + CH * DM
        assert FFN_W == KC * QKVW and G * DM <= FFN_W
        fac_raw = {k: sb(f"fac_raw_{k}", [2 * P])[0:STACK, :] for k in KINDS}
        fac = {k: sb(f"fac_{k}", [2 * P], F32R)[0:STACK, :] for k in KINDS}
        fix = sb("fix", [2 * DM], F32R)[0:STACK, :]

        def weight_room(name, stack=ctx):
            return (sb(f"raw_{name}", [FFN_W], F32, stack), sb(f"w_h_{name}", [FFN_W], F32R, stack),
                    sb(f"w_l_{name}", [FFN_W], F32R, stack))

        late_room = weight_room("late")

        own_last = [None]

        def own_step(instruction):
            own_last[0] = own.mark(instruction)

        def own_wait():
            own.wait(dve, own_last[0])

        def inverse_root(mean_square, eps, n, scale=1.0):
            m, y, a, b = (t[:, 0:n] for t in (root_m, root_y, root_a, root_b))
            own_wait()
            yield own_step(dve.tensor_scalar(m, mean_square, scale, eps, ALU.mult, ALU.add))
            own_wait()
            yield own_step(dve.tensor_scalar(y.bitcast(I32), m.bitcast(I32), -0.5, ROOT_MAGIC, ALU.mult, ALU.add))
            for newton in range(NEWTONS):
                own_wait()
                yield own_step(dve.scalar_tensor_tensor(a, y, -0.5, y, ALU.mult, ALU.mult))
                own_wait()
                yield own_step(dve.tensor_tensor(b, a, m, ALU.mult))
                own_wait()
                last = dve.scalar_tensor_tensor(y, b, 1.5, y, ALU.add, ALU.mult)
                yield own_step(last) if newton < NEWTONS - 1 else last

        def matmul3(bank, left, right, first, last):
            (lh, ll), (rh, rl) = left, right
            pe.matmul(bank, lh, rh, start=first, stop=False)
            pe.matmul(bank, lh, rl, start=False, stop=False)
            return pe.matmul(bank, ll, rh, start=False, stop=last)

        def split_result(n, src, hi, lo, scale=None, spare=0):
            full.wait(act, n)
            if scale is None:
                hi_done.mark(act.copy(hi, src))
            else:
                hi_done.mark(act.activation(hi, src, ACT.Copy, scale=scale))
            hi_done.wait(dve)
            if scale is None:
                last = dve.tensor_tensor(lo, src, hi.bitcast(F32), ALU.subtract)
            else:
                last = dve.scalar_tensor_tensor(lo, src, scale, hi.bitcast(F32), ALU.mult, ALU.subtract)
            return evac.mark(last, spare=spare)

        row_read, xn_ready = {}, {}

        def statistics(t):
            evac.wait(dve)
            own_step(dve.bn_stats(stats[:, t, :], xr[:, t, :]))

        def normalize(b):
            blocks = slice(b * TB, (b + 1) * TB)
            own_wait()
            for t in range(B * TB)[blocks]:
                last = dve.bn_aggr(mv[:, t, :], stats[:, t, :])
                yield
            own_step(last)
            rows_done.wait(dve)
            for last in inverse_root(mv[:, blocks, 1], LN_EPS, TB):
                yield
            own_step(last)
            own_wait()
            if b in row_read:
                full.wait(dve, row_read[b])
            for t in range(TB):
                xn_done.mark(dve.tensor_scalar(xn[:, b, t, :], xr[:, b * TB + t, :], mv[:, b * TB + t, 0:1], root_y[:, t:t + 1],
                                               ALU.subtract, ALU.mult))
                yield

        def finish(steps):
            for _ in steps:
                pass

        def turn_normed(b, blocks=range(TB)):
            for t in blocks:
                xn_done.wait(pe, Mark(xn_done.count - TB + t + 1))
                bank = next_bank()
                for k in range(KC):
                    last = pe.transpose(bank[:, k * P:(k + 1) * P], xn[:, b, t, k * P:(k + 1) * P], ident[:, :])
                row_read[b] = full.mark(last)
                cols = slice(b * S + t * P, b * S + (t + 1) * P)
                xn_ready[b] = split_result(row_read[b], bank[:, :].rearrange("p (k c) -> p k c", k=KC),
                                           xnT_hi[:, :, cols], xnT_lo[:, :, cols])

        lo_rows = sb("lo_rows", [2])[0:STACK, :]
        LEFT, RIGHT = lo_rows[:, 0:1], lo_rows[:, 1:2]
        fac_ready, w_ready = {}, {}

        def split_factor(raw, stack, parts):
            for cols, lo in parts:
                last = act.activation(stack[:, cols], raw[:, cols], ACT.Copy, scale=lo)
            fac_hi.mark(last)
            fac_hi.wait(pool)
            return fac_done.mark(pool.tensor_tensor(stack[:, :], raw[:, :], stack[:, :].bitcast(F32), ALU.subtract))

        def stack_factors(kind):
            fac_in[kind].wait(act)
            full.wait(act)
            fac_ready[kind] = split_factor(fac_raw[kind], fac[kind], [(slice(0, 2 * P), LEFT if kind == "down" else RIGHT)])

        def load_ffn(room, kind, step):
            at = slice(step, step + 1) if isinstance(step, int) else bass.ds(step, 1)
            w_lo.wait(sp)
            settle(sp)
            fac_done.wait(sp)
            settle(sp)
            cols = slice(START[kind], START[kind] + COLS[kind])
            fac_in[kind].mark(sp.dma_start(fac_raw[kind], ffn_fac[at][:, KINDS.index(kind)].rearrange("s r c -> r (s c)")), 16)
            w_in[kind].mark(sp.dma_start(room[0][:, cols], ffn_w[at][:, :, cols].rearrange("s p c -> p (s c)")), 16)

        def scale_weights(room, kind, spare=0):
            raw, w_h, w_l = room
            fac_done.wait(pe, fac_ready[kind])
            for half in range(2):
                bank = next_bank()
                if kind == "down":
                    last = pe.matmul(bank[:, :], fac[kind][:, half * P:(half + 1) * P], fix[:, DM:2 * DM], start=True, stop=True)
                else:
                    for n in range(KC // 2):
                        k = half * (KC // 2) + n
                        last = pe.matmul(bank[:, n * 2 * P:(n + 1) * 2 * P], fix[:, k * P:(k + 1) * P], fac[kind],
                                         start=True, stop=True, skip_group_check=True)
                n = full.mark(last, spare=spare * half)
                cols = slice(START[kind] + half * DM, START[kind] + (half + 1) * DM)
                w_in[kind].wait(dve)
                full.wait(dve, n)
                evac.mark(dve.tensor_tensor(raw[:, cols], bank[:, :], raw[:, cols], ALU.mult), spare=spare * half)
                evac.wait(act)
                w_hi.mark(act.copy(w_h[:, cols], raw[:, cols]))
                w_hi.wait(pool)
                w_ready[kind] = w_lo.mark(pool.tensor_tensor(w_l[:, cols], raw[:, cols], w_h[:, cols].bitcast(F32),
                                                             ALU.subtract))

        def ffn(tag, room, prepare, finished, last_part):
            with ExitStack() as part_memory:
                def psb(name, shape, dt=F32):
                    return sb(name + tag, shape, dt, part_memory)

                silu = psb("silu", [CH, S])
                d = psb("d", [CH, S])
                d_hi = psb("d_hi", [CH, B, S], F32R)
                d_lo = psb("d_lo", [CH, B, S], F32R)
                w_h, w_l = room[1:]
                d_ready = {}

                def gate_up(c, b):
                    kind = f"gu{c}"
                    w_lo.wait(pe, w_ready[kind])
                    results = []
                    for half in range(2):
                        bank = next_bank(xn_ready[b])
                        for k in range(KC):
                            w = START[kind] + (2 * k + half) * P
                            w = slice(w, w + P)
                            tokens = slice(b * S, (b + 1) * S)
                            last = matmul3(bank[:, :], (w_h[:, w], w_l[:, w]),
                                           (xnT_hi[:, k, tokens], xnT_lo[:, k, tokens]), k == 0, k == KC - 1)
                        results.append((full.mark(last), bank))
                    (n_a, bank_a), (n_b, bank_b) = results
                    full.wait(act, n_a)
                    hi_done.mark(act.activation(silu[:, c, :], bank_a[:, :], ACT.Silu))
                    hi_done.wait(dve)
                    full.wait(dve, n_b)
                    gated.mark(dve.tensor_tensor(d[:, c, :], bank_b[:, :], silu[:, c, :], ALU.mult))
                    gated.wait(act)
                    hi_done.mark(act.copy(d_hi[:, c, b, :], d[:, c, :]))
                    hi_done.wait(dve)
                    d_ready[b] = evac.mark(dve.tensor_tensor(d_lo[:, c, b, :], d[:, c, :], d_hi[:, c, b, :].bitcast(F32),
                                                             ALU.subtract), 2)

                def down(b, ends):
                    w_lo.wait(pe, w_ready["down"])
                    for t in range(TB):
                        bank = next_bank(d_ready[b])
                        tokens = slice(t * P, (t + 1) * P)
                        for c in range(CH):
                            w = START["down"] + c * DM
                            w = slice(w, w + DM)
                            last = matmul3(bank[:, :], (d_hi[:, c, b, tokens], d_lo[:, c, b, tokens]),
                                           (w_h[:, w], w_l[:, w]), c == 0, c == CH - 1)
                        full.wait(dve, full.mark(last))
                        row = xr[:, b * TB + t, :]
                        evac.mark(dve.scalar_tensor_tensor(row, bank[:, :], 0.5, row, ALU.mult, ALU.add))
                        if ends:
                            finished(b * TB + t)

                def step(i, more):
                    if more:
                        for kind in KINDS:
                            load_ffn(room, kind, i + 1)
                    gate_up(1, 0)
                    if more:
                        stack_factors("gu0")
                    gate_up(0, 1)
                    if more:
                        scale_weights(room, "gu0")
                    if last_part and not more:
                        gate_up(1, 1)
                        down(0, True)
                        down(1, True)
                        return
                    down(0, not more)
                    if more:
                        stack_factors("gu1")
                    else:
                        finish(normalize(0))
                    gate_up(1, 1)
                    if more:
                        scale_weights(room, "gu1")
                        stack_factors("down")
                        gate_up(0, 0)
                    else:
                        turn_normed(0)
                    down(1, not more)
                    if more:
                        scale_weights(room, "down", FFN_SPARE)

                finish(normalize(1))
                gate_up(0, 0)
                turn_normed(1)
                with loop("ffn", STEPS - 1) as i:
                    step(i, True)
                prepare()
                step(STEPS - 1, False)

        qkv_room = [t[:, 0:KC * QKVW].rearrange("p (k c) -> p k c", k=KC) for t in late_room]
        o_raw = late_room[0][:, 0:G * DM].rearrange("p (k c) -> p k c", k=G)
        bias_ready = {}

        def load_attention(kind, step):
            at = slice(step, step + 1) if isinstance(step, int) else bass.ds(step, 1)
            w_lo.wait(sp)
            settle(sp)
            src, chunks = (w_qkv, KC * QKVW) if kind == "qkv" else (w_o, G * DM)
            w_in[kind].mark(sp.dma_start(late_room[0][:, 0:chunks], src[at].rearrange("s p c -> p (s c)")), 16)

        def split_weights(kind, raw, hi, lo):
            read = Mark(full.count)

            def chunks():
                w_in[kind].wait(act)
                full.wait(act, read)
                for k in range(KC if kind == "qkv" else G):
                    w_hi.mark(act.copy(hi[:, k, :], raw[:, k, :]))
                    w_hi.wait(pool)
                    w_ready[kind] = w_lo.mark(pool.tensor_tensor(lo[:, k, :], raw[:, k, :], hi[:, k, :].bitcast(F32),
                                                                 ALU.subtract))
                    yield

            return chunks()

        def first_biases(distance):
            bias_done.mark(pool.iota(distance[:, :], pattern=[[1, S]], base=-(S - P), channel_multiplier=-1))
            bias_done.wait(pool)
            for h in range(G):
                bias_done.mark(pool.tensor_scalar(bias[:, h, :], distance[:, :], float(np.float32(SLOPE0 ** (h + 1))), None, ALU.mult))
            bias_done.wait(pool)
            for h in range(G):
                bias_ready[h] = bias_done.mark(pool.affine_select(
                    out=bias[:, h, :], in_=bias[:, h, :], compare_op=ALU.is_ge, fill=MASKED, base=S - P,
                    pattern=[[-1, S]], channel_multiplier=1))

        def attention():
            with ExitStack() as part_memory:
                def psb(name, shape, dt=F32):
                    return sb(name, shape, dt, part_memory)

                _, qkv_h, qkv_l = qkv_room
                o_h, o_l = psb("o_h", [G, DM], F32R), psb("o_l", [G, DM], F32R)
                o_room = (o_raw, o_h, o_l)
                square = psb("square", [G + 1, HD])
                sums = psb("sums", [TB, G + 1])
                v_h, v_l = psb("v_h", [B, TB, HD], F32R), psb("v_l", [B, TB, HD], F32R)
                kT_h, kT_l = psb("kT_h", [B, S], F32R), psb("kT_l", [B, S], F32R)
                qT_h, qT_l = psb("qT_h", [2, S], F32R), psb("qT_l", [2, S], F32R)
                OFF = [P * i * (i + 1) // 2 for i in range(TB + 1)]
                prob = psb("prob", [2, OFF[TB]])
                probT_h, probT_l = psb("probT_h", [OFF[TB]], F32R), psb("probT_l", [OFF[TB]], F32R)
                oT_h, oT_l = psb("oT_h", [2, 2, S], F32R), psb("oT_l", [2, 2, S], F32R)
                top, neg_top, total, inverse = (psb(n, [2, TB]) for n in ("top", "neg_top", "total", "inverse"))
                TURNS = [[(0, 0)], [(1, 0), (3, 3 * P)], [(2, 0)]]
                probT_at = {j: S * n + at for n, turn in enumerate(TURNS) for j, at in turn}
                assert len(TURNS) == PROB_RESULTS and TB == 4
                rows_ready, oT_ready, row_summed, q_ready, probT_ready = {}, {}, {}, [None], [None]

                def project(b, t):
                    w_lo.wait(pe, w_ready["qkv"])
                    results = []
                    tokens = slice(b * S + t * P, b * S + (t + 1) * P)
                    for cols in (slice(0, QW), slice(QW, QKVW)):
                        bank = next_bank(xn_ready[b])
                        for k in range(KC):
                            last = matmul3(bank[:, 0:cols.stop - cols.start], (xnT_hi[:, k, tokens], xnT_lo[:, k, tokens]),
                                           (qkv_h[:, k, cols], qkv_l[:, k, cols]), k == 0, k == KC - 1)
                        results.append((full.mark(last), bank))
                    (n_q, bank_q), (n_kv, bank_kv) = results
                    q, k = rows[:, b, t, 0:G, :], rows[:, b, t, G, :]
                    bank_q = bank_q[:, :].rearrange("p (h d) -> p h d", h=G)
                    full.wait(act, n_q)
                    q_copied = hi_done.mark(act.copy(q, bank_q))
                    full.wait(act, n_kv)
                    hi_done.mark(act.copy(k, bank_kv[:, 0:HD]))
                    hi_done.mark(act.copy(v_h[:, b, t, :], bank_kv[:, HD:2 * HD]))
                    own_wait()
                    hi_done.wait(dve, q_copied)
                    evac.mark(dve.tensor_tensor(square[:, 0:G, :], bank_q, q, ALU.mult))
                    hi_done.wait(dve)
                    dve.tensor_tensor(v_l[:, b, t, :], bank_kv[:, HD:2 * HD], v_h[:, b, t, :].bitcast(F32), ALU.subtract)
                    evac.mark(dve.tensor_tensor(square[:, G, :], bank_kv[:, 0:HD], k, ALU.mult))
                    evac.wait(dve)
                    own_step(dve.tensor_reduce(sums[:, t, :], square[:, :, :], AX.X, ALU.add))

                def row_roots():
                    rows_done.wait(dve)
                    for last in inverse_root(sums[:, :, :].rearrange("p t h -> p (t h)"), RMS_EPS, ROOTS, 1.0 / HD):
                        yield
                    root_done.mark(last)

                def norm_rows(b):
                    root_done.wait(act)
                    root = root_y[:, :].rearrange("p (t h) -> p t h", h=G + 1)
                    for t in range(TB):
                        last = act.activation(rows[:, b, t, G, :], rows[:, b, t, G, :], ACT.Copy, scale=root[:, t, G:G + 1])
                    k_done.mark(last)
                    root_done.wait(pool)
                    for head in range(G):
                        by = root[:, :, head].unsqueeze(2).to_broadcast([P, TB, HD])
                        rows_ready[head] = rows_done.mark(pool.tensor_tensor(rows[:, b, :, head], rows[:, b, :, head], by, ALU.mult))

                def turn_rows(b, head, hi, lo, weight, spare=0):
                    if head == G:
                        k_done.wait(pe)
                    else:
                        rows_done.wait(pe, rows_ready[head])
                    bank = next_bank()
                    for t in range(TB):
                        last = pe.transpose(bank[:, t * P:(t + 1) * P], rows[:, b, t, head, :], ident[:, :])
                    row_read[b] = full.mark(last, spare=spare)
                    return split_result(row_read[b], bank[:, :], hi, lo, weight, spare)

                def turn_k(b):
                    turn_rows(b, G, kT_h[:, b, :], kT_l[:, b, :], wkcol[:, 0:1])

                def turn_q(b, h, spare=0):
                    q_ready[0] = turn_rows(b, h, qT_h[:, h % 2, :], qT_l[:, h % 2, :], wcol[:, 0:1], spare)

                def scores(b, h):
                    s = h % 2
                    for i in range(TB):
                        bank = next_bank(q_ready[0])
                        n_keys = (i + 1) * P
                        q = slice(i * P, (i + 1) * P)
                        last = matmul3(bank[:, 0:n_keys], (qT_h[:, s, q], qT_l[:, s, q]),
                                       (kT_h[:, b, 0:n_keys], kT_l[:, b, 0:n_keys]), True, True)
                        full.wait(dve, full.mark(last))
                        bias_done.wait(dve, bias_ready[h])
                        settle(dve)
                        evac.mark(dve.tensor_tensor_reduce(
                            prob[:, s, OFF[i]:OFF[i + 1]], bank[:, 0:n_keys], bias[:, h, S - n_keys:S], 1.0, MASKED,
                            ALU.add, ALU.max, top[:, s, i:i + 1]))
                    evac.wait(dve)
                    top_done.mark(dve.tensor_scalar(neg_top[:, s, :], top[:, s, :], -1.0, None, ALU.mult))

                def exponentials(h):
                    s = h % 2
                    top_done.wait(act)
                    for i in range(TB):
                        p = prob[:, s, OFF[i]:OFF[i + 1]]
                        last = act.activation(p, p, ACT.Exp, bias=neg_top[:, s, i:i + 1], accum_out=total[:, s, i:i + 1])
                    exp_done.mark(last)

                def probabilities(h):
                    s = h % 2
                    exp_done.wait(dve)
                    own_step(dve.reciprocal(inverse[:, s, :], total[:, s, :]))
                    own_wait()
                    for i in range(TB):
                        p = prob[:, s, OFF[i]:OFF[i + 1]]
                        last = dve.tensor_scalar(p, p, inverse[:, s, i:i + 1], None, ALU.mult)
                    prob_done.mark(last)

                def turn_probabilities(h):
                    s = h % 2
                    prob_done.wait(pe)
                    for n, turn in enumerate(TURNS):
                        bank = next_bank()
                        for j, at in turn:
                            for i in range(j, TB):
                                here = at + (i - j) * P
                                last = pe.transpose(bank[:, here:here + P], prob[:, s, OFF[i] + j * P:OFF[i] + (j + 1) * P], ident[:, :])
                        width = here + P
                        here = slice(n * S, n * S + width)
                        probT_ready[0] = split_result(full.mark(last), bank[:, 0:width], probT_h[:, here], probT_l[:, here])

                def weigh_values(b, h):
                    bank = next_bank(probT_ready[0])
                    for j in range(TB):
                        width = S - j * P
                        here = slice(probT_at[j], probT_at[j] + width)
                        last = matmul3(bank[:, j * P:S], (v_h[:, b, j, :], v_l[:, b, j, :]),
                                       (probT_h[:, here], probT_l[:, here]), j == 0, j == TB - 1)
                    half = h // 2
                    oT_ready[half] = split_result(full.mark(last), bank[:, :], oT_h[:, half, h % 2, :], oT_l[:, half, h % 2, :])

                def project_out(b, half, blocks, spare=0, ends=False):
                    w_lo.wait(pe, w_ready["o"])
                    for t in blocks:
                        bank = next_bank(oT_ready[half])
                        tokens = slice(t * P, (t + 1) * P)
                        for n in range(2):
                            h = 2 * half + n
                            last = matmul3(bank[:, :], (oT_h[:, half, n, tokens], oT_l[:, half, n, tokens]),
                                           (o_h[:, h, :], o_l[:, h, :]), n == 0, n == 1)
                        spared = spare if t == blocks[-1] else 0
                        if (b, half, t) == (B - 1, 1, TB - 1):
                            evac.wait(dve, row_summed[t])
                        full.wait(dve, full.mark(last, spare=spared))
                        row = xr[:, b * TB + t, :]
                        row_summed[t] = evac.mark(dve.tensor_tensor(row, bank[:, :], row, ALU.add), spare=spared)
                        if ends:
                            statistics(b * TB + t)

                RESULTS_AFTER_Q = 1 + 1 + 1 + 1 + TB
                ROOT_STEPS_AHEAD = 6
                PROJECT = [(0, 1), (2,), (3,), ()]
                OUT = {3: (0, 0, (0, 1)), 4: (0, 0, (2, 3)), 5: (0, 1, (0, 1)), 6: (0, 1, (2, 3)), 7: (1, 0, (0, 1))}

                def group(g, more):
                    o_chunks, qkv_chunks = split_weights("o", *o_room), iter(())
                    roots = iter(())
                    spare = iter([1] * ATT_SPARE if more else [])
                    for pair in range(PAIRS):
                        b, h = divmod(pair, G)
                        next_b = 1 - b
                        projects = more or b == 0
                        early = h in (1, 2) and projects
                        if pair == G - 1:
                            finish(roots)
                        scores(b, h)
                        if pair == G and more:
                            finish(qkv_chunks)
                            load_attention("o", g + 1)
                        if pair:
                            turn_probabilities((h - 1) % G)
                        if pair == PAIRS - 1 and more:
                            finish(roots)
                        if h < G - 1:
                            turn_q(b, h + 1)
                        if pair != G - 1:
                            exponentials(h)
                        if h == G - 1 and projects:
                            norm_rows(next_b)
                        if b == B - 1 and more:
                            for head in {G - 1: (G - 2, G - 1)}.get(h, (h,) if h < G - 2 else ()):
                                evac.wait(pool)
                                settle(pool)
                                bias_ready[head] = bias_done.mark(pool.tensor_scalar(bias[:, head, :], bias[:, head, :], 0.5, None, ALU.mult))
                        if pair == PAIRS - 1:
                            probabilities(h)
                        if pair == 0:
                            next(o_chunks)
                            next(o_chunks)
                        if early:
                            probabilities(h)
                            for t in PROJECT[h]:
                                project(next_b, t)
                        if pair in OUT:
                            out_b, half, blocks = OUT[pair]
                            project_out(out_b, half, blocks, next(spare, 0), not more and (out_b, half) == (0, 1))
                        if pair == G - 1:
                            turn_k(next_b)
                            turn_q(next_b, 0)
                            exponentials(h)
                        if not early and pair < PAIRS - 1:
                            probabilities(h)
                        if h == G - 2 and projects:
                            roots = row_roots()
                            for _ in range(ROOT_STEPS_AHEAD):
                                next(roots)
                        if pair:
                            weigh_values(*divmod(pair - 1, G))
                        if projects and not early:
                            for t in PROJECT[h]:
                                project(next_b, t)
                        if pair == 0:
                            finish(o_chunks)
                            if more:
                                load_attention("qkv", g + 1)
                            else:
                                for kind in KINDS:
                                    load_ffn(late_room, kind, 0)
                        if pair == G - 2 and more:
                            qkv_chunks = split_weights("qkv", *qkv_room)
                            next(qkv_chunks)
                            next(qkv_chunks)
                        if pair == G - 1:
                            next(qkv_chunks, None)
                        if not more and G - 1 <= pair < G - 1 + len(KINDS):
                            stack_factors(KINDS[pair - G + 1])
                        if not more and G <= pair < G + len(KINDS):
                            scale_weights(late_room, KINDS[pair - G])
                    if not more:
                        finish(normalize(0))
                    turn_probabilities(G - 1)
                    if more:
                        turn_k(0)
                        turn_q(0, 0)
                    project_out(B - 1, 0, (2,), next(spare, 0))
                    weigh_values(B - 1, G - 1)
                    if not more:
                        turn_normed(0)
                    project_out(B - 1, 0, (3,))
                    project_out(B - 1, 1, tuple(range(TB)), ends=not more)
                    assert not list(spare)

                bias_done.wait(act)
                bias_done.wait(dve)
                finish(normalize(1))
                for t in range(TB):
                    project(0, t)
                finish(row_roots())
                norm_rows(0)
                turn_normed(1, range(TB)[:TB // 2])
                turn_k(0)
                turn_q(0, 0, RESULTS_AFTER_Q - TB // 2)
                turn_normed(1, range(TB)[TB // 2:])
                ahead = evac.count - q_ready[0].count
                with loop("att", HKV - 1) as g:
                    group(g, True)
                    assert evac.count - q_ready[0].count == ahead
                group(HKV - 1, False)

        x_rows = x.rearrange("b (t p) c -> (b t) p c", p=P)
        out_rows = out.rearrange("b (t p) c -> (b t) p c", p=P)
        with ExitStack() as early_memory:
            early_room = weight_room("early", early_memory)
            fix_raw = sb("fix_raw", [2 * DM], F32, early_memory)[0:STACK, :]
            distance = sb("distance", [S], I32, early_memory)

            fix_in.mark(sp.dma_start(lo_rows, factor_lo), 16)
            fix_in.mark(sp.dma_start(fix_raw, ffn_fix), 16)
            for t in range(TB):
                x_in[t].mark(sp.dma_start(xr[:, t, :], x_rows[t]), 16)
            load_ffn(early_room, "gu0", 0)
            for t in range(TB, B * TB):
                x_in[t].mark(sp.dma_start(xr[:, t, :], x_rows[t]), 16)
            load_ffn(early_room, "gu1", 0)
            load_ffn(early_room, "down", 0)
            norm_in.mark(sp.dma_start(wcol[:, :], norm_w), 16)
            load_attention("qkv", 0)
            dve.sem_inc(evac.sem, BANKS)
            evac.count = BANKS
            ready.mark(pool.memset(ident[:, :], 0.0))
            ready.wait(pool)
            ready.mark(pool.affine_select(out=ident[:, :], in_=ident[:, :], compare_op=ALU.not_equal, fill=1.0,
                                          base=0, pattern=[[-1, P]], channel_multiplier=1))
            ready.wait(pe)
            for t in range(TB):
                x_in[t].wait(dve)
                statistics(t)
            finish(normalize(0))
            fix_in.wait(act)
            split_factor(fix_raw, fix, [(slice(0, DM), LEFT), (slice(DM, 2 * DM), RIGHT)])
            for kind in KINDS:
                stack_factors(kind)
            scale_weights(early_room, "gu0")
            turn_normed(0)
            scale_weights(early_room, "gu1")
            scale_weights(early_room, "down")
            for t in range(TB, B * TB):
                x_in[t].wait(dve)
                statistics(t)

            def prepare_attention():
                finish(split_weights("qkv", *qkv_room))
                load_attention("o", 0)
                first_biases(distance)

            ffn("_1", early_room, prepare_attention, statistics, False)
        norm_in.wait(dve)
        own_step(dve.tensor_scalar(wkcol[:, :], wcol[:, 1:2], float(HD) ** -0.5, None, ALU.mult))
        attention()

        def store(t):
            evac.wait(sp)
            x_out.mark(sp.dma_start(out_rows[t], xr[:, t, :]), 16)

        ffn("_2", late_room, lambda: None, store, True)
        x_out.wait(sp)


def kernel(**inputs):
    import concourse.bacc as bacc
    from concourse.bass_utils import run_bass_kernel_spmd

    a = {k.removeprefix("L0_"): np.asarray(v) for k, v in inputs.items()}

    def rows_by_chunk(wt, chunk):
        k = wt.shape[0] // P
        return wt.reshape(k, P, -1, chunk).transpose(2, 1, 0, 3).reshape(-1, P, k * chunk)

    gate, up = (rows_by_chunk(a[f"ffn_{n}_w"].T, P).reshape(STEPS, CH, P, KC, P) for n in ("gate", "up"))
    gate_up = np.concatenate([gate, up], axis=4).reshape(STEPS, CH, P, 2 * KC * P)
    down = a["ffn_down_w"].T.reshape(STEPS, CH, P, DM)
    ffn_w = np.concatenate([gate_up[:, c] for c in range(CH)] + [down[:, c] for c in range(CH)], axis=2)
    su_g, su_u = (a[f"ffn_{n}_su"].T.reshape(R, STEPS, CH, P) for n in ("gate", "up"))
    sv_d = a["ffn_down_sv"].reshape(R, STEPS, CH * P)
    half = STACK // 2
    ffn_fac = np.zeros((STEPS, CH + 1, STACK, 2 * P), np.float32)
    four = lambda t: np.tile(t, (1, half // R, 1))
    for c in range(CH):
        ffn_fac[:, c, :half, :P] = four(su_g[:, :, c].transpose(1, 0, 2))
        ffn_fac[:, c, half:, P:] = four(su_u[:, :, c].transpose(1, 0, 2))
    ffn_fac[:, CH, :half] = four(sv_d.transpose(1, 0, 2))
    ffn_fix = np.zeros((STACK, 2 * DM), np.float32)
    ffn_fix[:half, :DM], ffn_fix[half:, :DM] = (np.tile(a[f"ffn_{n}_sv"], (half // R, 1)) for n in ("gate", "up"))
    ffn_fix[:half, DM:] = np.tile(a["ffn_down_su"].T, (half // R, 1))
    place = np.arange(STACK) % half // R
    factor_lo = np.stack([place // 2, place % 2], axis=1).astype(np.float32)
    q = a["attn_Wq"].T.reshape(KC, P, HKV, QW)
    k, v = (a[f"attn_{n}"].T.reshape(KC, P, HKV, HD) for n in ("Wk", "Wv"))
    w_qkv = np.concatenate([q, k, v], axis=3).transpose(2, 1, 0, 3).reshape(HKV, P, KC * QKVW)
    w_o = a["attn_Wo"].T.reshape(HKV, G, P, DM).transpose(0, 2, 1, 3).reshape(HKV, P, G * DM)
    norm_w = np.stack([a["attn_q_norm_w"], a["attn_k_norm_w"]], axis=1)
    arrays = {"x": a["attn_x"], "ffn_w": ffn_w, "ffn_fac": ffn_fac, "ffn_fix": ffn_fix, "factor_lo": factor_lo,
              "w_qkv": w_qkv, "w_o": w_o, "norm_w": norm_w}
    arrays = {name: np.ascontiguousarray(v) for name, v in arrays.items()}

    nc = bacc.Bacc("TRN2", target_bir_lowering=False, num_devices=1)
    args = [nc.dram_tensor(name, v.shape, mybir.dt.from_np(v.dtype), kind="ExternalInput").ap() for name, v in arrays.items()]
    args.append(nc.dram_tensor("y", (B, S, DM), F32, kind="ExternalOutput").ap())
    build(nc, *args)
    return run_bass_kernel_spmd(nc, [arrays], core_ids=[0]).results[0]["y"]
```
